# Optimizing a Trainium2 kernel written in Bass

```python
import numpy as np
import jax
import jax.numpy as jnp

def _softmax(x, axis=-1):
    return jax.nn.softmax(x, axis=axis)

def _gelu(x):
    return jax.nn.gelu(x, approximate=True)

def _silu(x):
    return jax.nn.silu(x)

def _sigmoid(x):
    return jax.nn.sigmoid(x)

def _layernorm(x, axis=-1, eps=1e-05):
    m = jnp.mean(x, axis=axis, keepdims=True)
    v = jnp.var(x, axis=axis, keepdims=True)
    return (x - m) / jnp.sqrt(v + eps)

def _scatter_add(tgt, idx, src, axis=0):
    return tgt.at[idx].add(src)

def _segment_sum(src, seg, n):
    return jax.ops.segment_sum(src, seg, n)
kernel_name = 'mk_adaln_ffn_d1_seqx_r4_062ded'

def setup_inputs(seed: int=0):
    np.random.seed(seed)
    _w = jnp.asarray

    def _rec_inputs():
        import jax
        import jax.numpy as jnp
        _rk = jax.random.key(seed)
        x = -0.0002071 + 1 * jax.random.normal(jax.random.fold_in(_rk, 1), (64, 64, 256), jnp.float32)
        _lenS = 64 - jax.random.randint(jax.random.fold_in(_rk, 7), (64,), 0, max(1, 64 // 4) + 1, jnp.int32)
        _lenS2 = 64 - jax.random.randint(jax.random.fold_in(_rk, 8), (64,), 0, max(1, 64 // 4) + 1, jnp.int32)
        cond_8 = jax.random.uniform(jax.random.fold_in(_rk, 11), (64, 8), jnp.float32, 0.0, 0.983423)
        return (x, cond_8)
    x, cond_8 = _rec_inputs()

    def _L0_cond_setup():
        import jax, jax.numpy as jnp
        import numpy as np
        R = 16
        ALPHA = 32.0
        SCALING = ALPHA / R
        key = jax.random.key(seed)
        ks = jax.random.split(key, 6)
        B, T, C, O, E = (16, 375, 256, 256, 8)
        x = jax.random.normal(ks[0], (B, T, C), dtype=jnp.float32)
        w = jax.random.uniform(ks[1], (B, E), dtype=jnp.float32)
        W_base = jax.random.normal(ks[2], (O, C), dtype=jnp.float32) * 0.02
        b_base = jax.random.normal(ks[3], (O,), dtype=jnp.float32) * 0.02
        As = jax.random.normal(ks[4], (E, R, C), dtype=jnp.float32) * 0.02
        Bs = jax.random.normal(ks[5], (E, O, R), dtype=jnp.float32) * 0.02
        return {'x': x, 'w': w, 'W_base': W_base, 'b_base': b_base, 'As': As, 'Bs': Bs}
    _L0_cond_all = _L0_cond_setup()
    _L0_cond_in = {k: v for k, v in _L0_cond_all.items() if k in ('W_base', 'b_base', 'As', 'Bs')}
    del _L0_cond_all

    def _L0_ffn_setup():
        import jax, jax.numpy as jnp
        import numpy as np
        B, S, D = (1, 512, 256)
        E, K, F = (8, 2, 352)
        NS = 2
        SCALE = 2.5

        def _swiglu_mlp(x, wg, wu, wd):
            return jax.nn.silu(x @ wg) * (x @ wu) @ wd
        key = jax.random.key(seed)
        ks = jax.random.split(key, 8)
        s = 0.02
        return {'hidden_states': jax.random.normal(ks[0], (B, S, D), jnp.float32), 'gate_w': jax.random.normal(ks[1], (E, D), jnp.float32) * s, 'w_gate': jax.random.normal(ks[2], (E, D, F), jnp.float32) * s, 'w_up': jax.random.normal(ks[3], (E, D, F), jnp.float32) * s, 'w_down': jax.random.normal(ks[4], (E, F, D), jnp.float32) * s, 'sw_gate': jax.random.normal(ks[5], (D, F * NS), jnp.float32) * s, 'sw_up': jax.random.normal(ks[6], (D, F * NS), jnp.float32) * s, 'sw_down': jax.random.normal(ks[7], (F * NS, D), jnp.float32) * s}
    _L0_ffn_all = _L0_ffn_setup()
    _L0_ffn_in = {k: v for k, v in _L0_ffn_all.items() if k in ('gate_w', 'w_gate', 'w_up', 'w_down', 'sw_gate', 'sw_up', 'sw_down')}
    del _L0_ffn_all
    return {'x': x, 'cond_8': cond_8, 'L0_cond_W_base': _L0_cond_in['W_base'], 'L0_cond_b_base': _L0_cond_in['b_base'], 'L0_cond_As': _L0_cond_in['As'], 'L0_cond_Bs': _L0_cond_in['Bs'], 'L0_ffn_gate_w': _L0_ffn_in['gate_w'], 'L0_ffn_w_gate': _L0_ffn_in['w_gate'], 'L0_ffn_w_up': _L0_ffn_in['w_up'], 'L0_ffn_w_down': _L0_ffn_in['w_down'], 'L0_ffn_sw_gate': _L0_ffn_in['sw_gate'], 'L0_ffn_sw_up': _L0_ffn_in['sw_up'], 'L0_ffn_sw_down': _L0_ffn_in['sw_down']}

def reference(x, cond_8, L0_cond_W_base, L0_cond_b_base, L0_cond_As, L0_cond_Bs, L0_ffn_gate_w, L0_ffn_w_gate, L0_ffn_w_up, L0_ffn_w_down, L0_ffn_sw_gate, L0_ffn_sw_up, L0_ffn_sw_down):
    import jax
    import jax.numpy as jnp

    def _L0_cond_ref(x, w, W_base, b_base, As, Bs):
        import jax, jax.numpy as jnp
        import numpy as np
        R = 16
        ALPHA = 32.0
        SCALING = ALPHA / R
        out = jnp.einsum('btc,oc->bto', x, W_base) + b_base
        h = jnp.einsum('btc,erc->bter', x, As)
        lora = jnp.einsum('bter,eor,be->bto', h, Bs, w)
        return out + lora * SCALING

    def _L0_ffn_ref(hidden_states, gate_w, w_gate, w_up, w_down, sw_gate, sw_up, sw_down):
        import jax, jax.numpy as jnp
        import numpy as np
        B, S, D = (1, 512, 256)
        E, K, F = (8, 2, 352)
        NS = 2
        SCALE = 2.5

        def _swiglu_mlp(x, wg, wu, wd):
            return jax.nn.silu(x @ wg) * (x @ wu) @ wd
        identity = hidden_states
        x = hidden_states.reshape(-1, hidden_states.shape[-1])
        T = x.shape[0]
        logits = x.astype(jnp.float32) @ gate_w.astype(jnp.float32).T
        scores = jax.nn.softmax(logits, axis=-1)
        topk_w, topk_i = jax.lax.top_k(scores, K)
        topk_w = topk_w / (topk_w.sum(-1, keepdims=True) + 1e-20) * SCALE
        combine = jnp.zeros((T, E), jnp.float32).at[jnp.arange(T)[:, None], topk_i].set(topk_w)
        g = jax.nn.silu(jnp.einsum('td,edf->etf', x, w_gate)) * jnp.einsum('td,edf->etf', x, w_up)
        expert_out = jnp.einsum('etf,efd->etd', g, w_down)
        y = jnp.einsum('te,etd->td', combine, expert_out).astype(x.dtype)
        y = y.reshape(identity.shape)
        return y + _swiglu_mlp(identity, sw_gate, sw_up, sw_down)
    x = x + _L0_ffn_ref(_L0_cond_ref(x, cond_8, L0_cond_W_base, L0_cond_b_base, L0_cond_As, L0_cond_Bs), L0_ffn_gate_w, L0_ffn_w_gate, L0_ffn_w_up, L0_ffn_w_down, L0_ffn_sw_gate, L0_ffn_sw_up, L0_ffn_sw_down)
    return x

_drawn_inputs = setup_inputs


def setup_inputs(seed=0):
    import zlib

    import numpy as np

    out = dict(_drawn_inputs(seed))
    spreads = {}
    factors = {}
    for name, (base, spread) in spreads.items():
        noise = np.random.default_rng([zlib.crc32(name.encode()), seed]).standard_normal(out[name].shape)
        drawn = base * np.exp(spread * noise) if base else spread * noise
        out[name] = jnp.asarray(drawn.astype(out[name].dtype))
    for name, factor in factors.items():
        out[name] = (out[name] * factor).astype(out[name].dtype)
    return out
```

```python
from contextlib import ExitStack

import concourse.bass as bass
from concourse import mybir

F32 = mybir.dt.float32
F32R = mybir.dt.float32r
BF16 = mybir.dt.bfloat16
I32 = mybir.dt.int32
U32 = mybir.dt.uint32
ALU = mybir.AluOpType
ACT = mybir.ActivationFunctionType
AX = mybir.AxisListType

P = 128
TOPK = 2
LORA_SCALING = 2.0
ROUTED_SCALE = 2.5


def adaln_moe(nc, x, cond, w_base, b_base, lora_a, lora_b, gate_w, w_gate, w_up, w_down,
              sw_gate, sw_up, sw_down, out):
    NB, SEQ, D = x.shape
    E, RANK, _ = lora_a.shape
    F = w_gate.shape[2]
    T = NB * SEQ
    NT = T // P
    K = D // P
    ER = E * RANK
    NS = sw_gate.shape[1] // F
    NE = E + NS
    FULL = F // P
    REST = F - FULL * P
    FC = FULL + 1
    NBLK = (TOPK * T + E * (P - 1)) // P
    NBLKP = NBLK + NBLK % 2
    assert SEQ * 2 == P and K == 2 and ER == P and NS == 2 and E == 8 and REST > 0

    x_rows = x.rearrange("b s d -> (b s) d")
    out_rows = out.rearrange("b s d -> (b s) d")
    x1_dram = nc.dram_tensor("x1_rows", (T, D), F32, kind="Internal").ap()
    y_dram = nc.dram_tensor("y_slots", (NBLK * P, D), F32, kind="Internal").ap()

    with ExitStack() as ctx:
        def sb(name, shape, dt=F32, where=ctx):
            return where.enter_context(nc.sbuf_tensor(name, shape, dt))

        def sem(name):
            return ctx.enter_context(nc.semaphore(name))

        bank = [ctx.enter_context(nc.psum_tensor(f"bank{i}", [P, 512], F32)) for i in range(8)]

        gu_h = sb("gu_h", [P, NE, K, 2 * F], F32R)
        gu_l = sb("gu_l", [P, NE, K, 2 * F], F32R)
        dn_h = sb("dn_h", [P, NE, FC, D], F32R)
        dn_l = sb("dn_l", [P, NE, FC, D], F32R)
        gu_raw = sb("gu_raw", [P, K, 2 * F])
        dn_raw = sb("dn_raw", [P, FC, D])
        ident = sb("ident", [P, P])
        spare = sb("spare", [1, 2])
        logits = sb("logits", [P, NT, E])
        top_w = [sb(f"top_w{c}", [P, NT]) for c in range(TOPK)]
        slot_i = sb("slot_i", [P, TOPK, NT], I32)
        perm_i = sb("perm_i", [P, NBLKP], I32)
        blk_e = sb("blk_e", [1, NBLKP], I32)

        with ExitStack() as one:
            wa_h = sb("wa_h", [P, K, D + ER], F32R, one)
            wa_l = sb("wa_l", [P, K, D + ER], F32R, one)
            b_h = sb("b_h", [P, D], F32R, one)
            b_l = sb("b_l", [P, D], F32R, one)
            gate_t = sb("gate_t", [P, K, E], F32, one)
            bias = sb("bias", [P, D], F32, one)
            w_tok = sb("w_tok", [P, NT, E], F32, one)
            base_raw = sb("base_raw", [P, K, D], F32, one)
            a_raw = sb("a_raw", [P, D], F32, one)
            b_raw = sb("b_raw", [P, K, ER], F32, one)
            g_raw = sb("g_raw", [E, D], F32, one)
            xin = [sb(f"xin{i}", [P, D], F32, one) for i in range(2)]
            xt_h = [sb(f"xt_h{i}", [P, D], F32R, one) for i in range(2)]
            xt_l = [sb(f"xt_l{i}", [P, D], F32R, one) for i in range(2)]
            hw = sb("hw", [P, ER], F32, one)
            hw_h = sb("hw_h", [P, P], F32R, one)
            hw_l = sb("hw_l", [P, P], F32R, one)
            x1 = [sb(f"x1_{i}", [P, D], F32, one) for i in range(2)]
            x1t = sb("x1t", [P, D], F32, one)
        with ExitStack() as two:
            R3 = [P, NT, E]
            prob = sb("prob", R3, F32, two)
            prob2 = sb("prob2", R3, F32, two)
            tmp = sb("tmp", R3, F32, two)
            hot = [sb(f"hot{c}", R3, F32, two) for c in range(TOPK)]
            mark = sb("mark", [P, NT + 1, E], BF16, two)
            pos = sb("pos", R3, F32, two)
            red = sb("red", [P, NT], F32, two)
            top_v = [sb(f"top_v{c}", [P, NT], F32, two) for c in range(TOPK)]
            down_e = sb("down_e", [P, E], F32, two)
            tri = sb("tri", [P, P], BF16, two)
            ones = sb("ones", [P, P], BF16, two)
            step128 = sb("step128", [P, NT], F32, two)
            over = sb("over", [P, E, NT], F32, two)
            upto = sb("upto", [P, E, E], F32, two)
            ee = sb("ee", [P, E, E], F32, two)
            nb = sb("nb", [P, E], F32, two)
            bend = sb("bend", [P, E], F32, two)
            bbase = sb("bbase", [P, E], F32, two)
            slot_f = sb("slot_f", [P, TOPK, NT], F32, two)
            part_i = sb("part_i", [P, TOPK, NT], I32, two)
            blk_of = sb("blk_of", [P, TOPK, NT], F32, two)
            row_of = sb("row_of", [P, TOPK, NT], F32, two)
            iota_row = sb("iota_row", [P, P], F32, two)
            iota_blk = sb("iota_blk", [P, NBLKP], F32, two)
            tok_id = sb("tok_id", [P, NT], F32, two)
            blk_cmp = sb("blk_cmp", [1, NBLKP, E], F32, two)
            blk_ef = sb("blk_ef", [1, NBLKP], F32, two)
            row_hot = [sb(f"row_hot{c}", [P, P], F32R, two) for c in range(TOPK)]
            blk_hot = [sb(f"blk_hot{c}", [P, NBLKP], F32R, two) for c in range(TOPK)]
        with ExitStack() as three:
            rows = [sb(f"rows{i}", [P, D], F32, three) for i in range(2)]
            rt_h = sb("rt_h", [P, D], F32R, three)
            rt_l = sb("rt_l", [P, D], F32R, three)
            act = sb("act", [P, F], F32, three)
            g = sb("g", [P, F], F32, three)
            gt_h = sb("gt_h", [P, FC * P], F32R, three)
            gt_l = sb("gt_l", [P, FC * P], F32R, three)
            y_sb = [sb(f"y_sb{i}", [P, D], F32, three) for i in range(2)]
            idx = [sb(f"idx{i}", [P, 1], I32, three) for i in range(2)]
            res = [sb(f"res{i}", [P, D], F32, three) for i in range(2)]
            pick = [[sb(f"pick{c}_{i}", [P, D], F32, three) for i in range(2)] for c in range(TOPK)]
            pidx = [[sb(f"pidx{c}_{i}", [P, 1], I32, three) for i in range(2)] for c in range(TOPK)]

        s_ident = sem("s_ident")
        s_const = sem("s_const")
        s_cw = sem("s_cw")
        s_wt = sem("s_wt")
        s_wth = sem("s_wth")
        s_wtl = sem("s_wtl")
        s_gu_raw = sem("s_gu_raw")
        s_dn_raw = sem("s_dn_raw")
        s_wdone = sem("s_wdone")
        s_pool = sem("s_pool")

        s_xin = [sem(f"s_xin{i}") for i in range(2)]
        s_tx, s_txh, s_txl = sem("s_tx"), sem("s_txh"), sem("s_txl")
        s_main, s_hw, s_thw = sem("s_main"), sem("s_hw"), sem("s_thw")
        s_hwh, s_hwl = sem("s_hwh"), sem("s_hwl")
        s_p, s_x1 = sem("s_p"), sem("s_x1")
        s_tx1, s_x1t, s_lg, s_lgc = sem("s_tx1"), sem("s_x1t"), sem("s_lg"), sem("s_lgc")
        s_x1st = [sem(f"s_x1st{i}") for i in range(2)]

        s_r, s_exp, s_rank, s_exp_in = sem("s_r"), sem("s_exp"), sem("s_rank"), sem("s_exp_in")
        s_mark = sem("s_mark")
        s_hot, s_permmm, s_routed = sem("s_hot"), sem("s_permmm"), sem("s_routed")
        s_warm = sem("s_warm")

        def ffn_sems(tag):
            names = "rt rth rtl G U act g gT gTh gTl D y".split()
            return {n: sem(f"{tag}_{n}") for n in names}

        fe, fs = ffn_sems("ex"), ffn_sems("sh")
        s_rows = [sem(f"s_rows{i}") for i in range(2)]
        s_yst = [sem(f"s_yst{i}") for i in range(2)]
        s_idx = sem("s_idx")
        s_srow = [sem(f"s_srow{i}") for i in range(2)]
        s_res = [sem(f"s_res{i}") for i in range(2)]
        s_pick = [sem(f"s_pick{i}") for i in range(2)]
        s_pidx = sem("s_pidx")
        s_mix = sem("s_mix")
        s_out = [sem(f"s_out{i}") for i in range(2)]

        block = ctx.enter_context(nc.Block())

        TX, MAIN, THW, TX1, LG = bank[0], bank[1:5], bank[5], bank[6], bank[7]
        XB, GB, UB, TB, YB = bank[0], bank[1], bank[2], bank[3], bank[4]

        def three_pass(pe, o, lh, ll, rh, rl, start, stop):
            pe.matmul(o, lh, rh, start=start, stop=False)
            pe.matmul(o, lh, rl, start=False, stop=False)
            return pe.matmul(o, ll, rh, start=False, stop=stop)

        def pairs(eng, lo, hi, step, n=2):
            turns = (hi - lo) // n
            if turns:
                with eng.Fori(0, turns) as j:
                    for u in range(n):
                        step(j * n + (lo + u), (lo + u) % n)
            for i in range(lo + n * turns, hi):
                step(i, i % n)

        def half_of(i, par):
            return i // 2 if isinstance(i, int) else (i - par % 2) // 2

        @block.sync
        def _(sp):
            sp.dma_start(base_raw[:], w_base.rearrange("(k p) c -> p k c", p=P)).then_inc(s_cw, 16)
            sp.dma_start(a_raw[:], lora_a.rearrange("e r c -> (e r) c")).then_inc(s_cw, 16)
            for k in range(K):
                sp.dma_start(b_raw[:, k, :].rearrange("p (e r) -> p e r", e=E),
                             lora_b[:, k * P:(k + 1) * P, :].rearrange("e o r -> o e r")).then_inc(s_cw, 16)
            sp.dma_start(g_raw[:], gate_w).then_inc(s_cw, 16)
            sp.dma_start(bias[:], b_base.rearrange("(a o) -> a o", a=1).broadcast_to([P, D])).then_inc(s_cw, 16)
            for h in range(2):
                sp.dma_start(w_tok[h * SEQ:(h + 1) * SEQ, :, :],
                             cond.rearrange("(a t h) e -> h a t e", a=1, h=2)[h].broadcast_to([SEQ, NT, E])
                             ).then_inc(s_cw, 16)

            def load_x(i, par):
                sp.dma_start(xin[par][:], x_rows[bass.ds(i * P, P), :]).then_inc(s_xin[par], 16)

            def store_x1(i, par):
                sp.wait_ge(s_x1, i + 1)
                sp.dma_start(x1_dram[bass.ds(i * P, P), :], x1[par][:]).then_inc(s_x1st[par], 16)

            load_x(0, 0)
            load_x(1, 1)

            def step_a(i, par):
                sp.wait_ge(s_tx, i - 1)
                load_x(i, par)
                store_x1(i - 2, par)
            pairs(sp, 2, NT, step_a)
            store_x1(NT - 2, NT % 2)
            store_x1(NT - 1, (NT - 1) % 2)

            def store_y(i, par):
                sp.wait_ge(fe["y"], i + 1)
                sp.dma_start(y_dram[bass.ds(i * P, P), :], y_sb[par][:]).then_inc(s_yst[par], 16)
            pairs(sp, 0, NBLK, store_y)

            def load_s(t, par):
                sp.dma_start(rows[par][:], x1_dram[bass.ds(t * P, P), :]).then_inc(s_srow[par], 16)
                sp.dma_start(res[par][:], x_rows[bass.ds(t * P, P), :]).then_inc(s_res[par], 16)

            def store_out(t, par):
                sp.wait_ge(fs["y"], t + 1)
                sp.dma_start(out_rows[bass.ds(t * P, P), :], y_sb[par][:]).then_inc(s_out[par], 16)

            load_s(0, 0)
            load_s(1, 1)

            def step_s(t, par):
                store_out(t - 2, par)
                load_s(t, par)
            pairs(sp, 2, NT, step_s)
            store_out(NT - 2, NT % 2)
            store_out(NT - 1, (NT - 1) % 2)
            for i in range(2):
                sp.wait_ge(s_out[i], 16 * (NT // 2))

        @block.gpsimd
        def _(pool):
            n_pool = [0]

            def before_dma():
                pool.tensor_tensor(spare[0:1, 1:2], spare[0:1, 0:1], spare[0:1, 0:1], ALU.add)

            def link(ins):
                n_pool[0] += 1
                ins.then_inc(s_pool, 1)
                pool.wait_ge(s_pool, n_pool[0])

            link(pool.memset(spare[:], 0.0))
            link(pool.memset(ident[:], 1.0))
            pool.affine_select(out=ident[:], in_=ident[:], compare_op=ALU.is_equal, fill=0.0, base=0,
                               pattern=[[-1, P]], channel_multiplier=1).then_inc(s_ident, 1)

            def load_gu(e):
                wg, wu = (w_gate, w_up) if not (isinstance(e, int) and e >= E) else (None, None)
                if wg is None:
                    c = (e - E) * F
                    g_src = sw_gate[:, c:c + F].rearrange("(k p) f -> p k f", p=P)
                    u_src = sw_up[:, c:c + F].rearrange("(k p) f -> p k f", p=P)
                else:
                    g_src = wg[bass.ds(e, 1)].rearrange("e (k p) f -> p (e k) f", p=P)
                    u_src = wu[bass.ds(e, 1)].rearrange("e (k p) f -> p (e k) f", p=P)
                pool.dma_start(gu_raw[:, :, 0:F], g_src).then_inc(s_gu_raw, 16)
                pool.dma_start(gu_raw[:, :, F:2 * F], u_src).then_inc(s_gu_raw, 16)

            def load_dn(e):
                if isinstance(e, int) and e >= E:
                    src = sw_down[(e - E) * F:(e - E + 1) * F, :]
                else:
                    src = w_down[bass.ds(e, 1)].rearrange("e f d -> (e f) d")
                pool.dma_start(dn_raw[:, 0:FULL, :],
                               src[0:FULL * P, :].rearrange("(c p) d -> p c d", p=P)).then_inc(s_dn_raw, 16)
                pool.dma_start(dn_raw[0:REST, FULL, :], src[FULL * P:F, :]).then_inc(s_dn_raw, 16)

            def split_parts(raw, hi, lo, count):
                pool.tensor_copy(hi, raw).then_inc(s_wdone, 1)
                pool.wait_ge(s_wdone, count)
                pool.tensor_tensor(lo, raw, hi.bitcast(F32), ALU.subtract).then_inc(s_wdone, 1)
                pool.wait_ge(s_wdone, count + 1)
                before_dma()

            def split_expert(e, n, nxt):
                def at(w, *rest):
                    v = w[(slice(None), bass.ds(e, 1)) + rest]
                    return v
                pool.wait_ge(s_gu_raw, n * 32 + 32)
                split_parts(gu_raw[:].rearrange("p k f -> p (k f)"),
                            gu_h[:, bass.ds(e, 1)].rearrange("p e k f -> p (e k f)"),
                            gu_l[:, bass.ds(e, 1)].rearrange("p e k f -> p (e k f)"), n * 6 + 1)
                if nxt is not None:
                    load_gu(nxt)
                pool.wait_ge(s_dn_raw, n * 32 + 32)
                split_parts(dn_raw[:, 0:FULL, :].rearrange("p c d -> p (c d)"),
                            dn_h[:, bass.ds(e, 1), 0:FULL, :].rearrange("p e c d -> p (e c d)"),
                            dn_l[:, bass.ds(e, 1), 0:FULL, :].rearrange("p e c d -> p (e c d)"), n * 6 + 3)
                split_parts(dn_raw[0:REST, FULL, :],
                            dn_h[0:REST, bass.ds(e, 1), FULL, :].rearrange("p e d -> p (e d)"),
                            dn_l[0:REST, bass.ds(e, 1), FULL, :].rearrange("p e d -> p (e d)"), n * 6 + 5)
                if nxt is not None:
                    load_dn(nxt)

            load_gu(0)
            load_dn(0)
            with pool.Fori(0, E - 1) as e:
                split_expert(e, e, e + 1)
            for e in range(E - 1, NE):
                split_expert(e, e, e + 1 if e + 1 < NE else None)

            pool.wait_ge(s_lgc, NT)
            for p in range(2):
                pool.wait_ge(s_x1st[p], 16 * (NT // 2))
            pool.iota(down_e[:], pattern=[[-1, E]], base=E, channel_multiplier=0,
                      allow_small_or_imprecise_dtypes=True)
            pool.iota(step128[:], pattern=[[P, NT]], base=0, channel_multiplier=0,
                      allow_small_or_imprecise_dtypes=True)
            pool.iota(iota_row[:], pattern=[[1, P]], base=0, channel_multiplier=0,
                      allow_small_or_imprecise_dtypes=True)
            pool.iota(iota_blk[:], pattern=[[1, NBLKP]], base=0, channel_multiplier=0,
                      allow_small_or_imprecise_dtypes=True)
            pool.iota(tok_id[:], pattern=[[P, NT]], base=0, channel_multiplier=1,
                      allow_small_or_imprecise_dtypes=True)
            pool.memset(ones[:], 1.0)
            link(pool.memset(tri[:], 1.0))
            link(pool.affine_select(out=tri[:], in_=tri[:], compare_op=ALU.is_gt, fill=0.0, base=0,
                                    pattern=[[1, P]], channel_multiplier=-1))
            link(pool.memset(upto[:], 1.0))
            link(pool.affine_select(out=upto[:], in_=upto[:], compare_op=ALU.is_ge, fill=0.0, base=0,
                                    pattern=[[1, E], [-1, E]], channel_multiplier=0))
            pool.memset(mark[:, NT, :], 0.0).then_inc(s_const, 1)

            pool.wait_ge(s_routed, 1)

            def gather(i, par, first=False):
                if not first:
                    pool.wait_ge(fe["rt"], i - 1)
                pool.tensor_copy(idx[par][:], perm_i[:, bass.ds(i, 1)]).then_inc(s_idx, 1)
                pool.wait_ge(s_idx, i + 1)
                before_dma()
                pool.indirect_dma_start(rows[par][:], None, x1_dram,
                                        bass.IndirectOffsetOnAxis(ap=idx[par][:, 0:1], axis=0)
                                        ).then_inc(s_rows[par], 16)
            gather(0, 0, True)
            gather(1, 1, True)
            pairs(pool, 2, NBLK, gather)

            pool.wait_ge(s_yst[0], 16 * ((NBLK + 1) // 2))
            pool.wait_ge(s_yst[1], 16 * (NBLK // 2))

            def gather_y(t, par, first=False):
                if not first:
                    pool.wait_ge(s_mix, t * 2 - 2)
                for c in range(TOPK):
                    pool.tensor_copy(pidx[c][par][:], slot_i[:, c, bass.ds(t, 1)]).then_inc(s_pidx, 1)
                    pool.wait_ge(s_pidx, t * 2 + (c + 1))
                    before_dma()
                    pool.indirect_dma_start(pick[c][par][:], None, y_dram,
                                            bass.IndirectOffsetOnAxis(ap=pidx[c][par][:, 0:1], axis=0)
                                            ).then_inc(s_pick[par], 16)
            gather_y(0, 0, True)
            gather_y(1, 1, True)
            pairs(pool, 2, NT, gather_y)

        def pe_turn_g(pe, s, i):
            pe.wait_ge(s["g"], i + 1)
            for c in range(FC):
                n = P if c < FULL else REST
                mm = pe.transpose(TB[0:n, c * P:(c + 1) * P], g[:, c * P:c * P + n], ident[:])
            mm.then_inc(s["gT"], 1)

        def pe_gate_up(pe, s, e, rows_ready):
            pe.wait_ge(s["rth"], rows_ready)
            pe.wait_ge(s["rtl"], rows_ready)
            for b, c, name in ((GB, 0, "G"), (UB, F, "U")):
                for k in range(K):
                    wh = gu_h[:, bass.ds(e, 1), k, c:c + F].rearrange("p e f -> p (e f)")
                    wl = gu_l[:, bass.ds(e, 1), k, c:c + F].rearrange("p e f -> p (e f)")
                    mm = three_pass(pe, b[:, 0:F], rt_h[:, k * P:(k + 1) * P], rt_l[:, k * P:(k + 1) * P],
                                    wh, wl, k == 0, k == K - 1)
                mm.then_inc(s[name], 1)

        def pe_turn_rows(pe, s, src):
            for k in range(K):
                mm = pe.transpose(XB[:, k * P:(k + 1) * P], src[:, k * P:(k + 1) * P], ident[:])
            mm.then_inc(s["rt"], 1)

        def pe_down(pe, s, i, e, start, stop):
            pe.wait_ge(s["gTh"], i + 1)
            pe.wait_ge(s["gTl"], i + 1)
            for c in range(FC):
                n = P if c < FULL else REST
                wh = dn_h[0:n, bass.ds(e, 1), c, :].rearrange("p e d -> p (e d)")
                wl = dn_l[0:n, bass.ds(e, 1), c, :].rearrange("p e d -> p (e d)")
                mm = three_pass(pe, YB[:, 0:D], gt_h[0:n, c * P:(c + 1) * P], gt_l[0:n, c * P:(c + 1) * P],
                                wh, wl, start and c == 0, stop and c == FC - 1)
            mm.then_inc(s["D"], 1)

        def act_gt(sc, s, i):
            sc.wait_ge(s["gT"], i + 1)
            sc.copy(gt_h[:, 0:FULL * P], TB[:, 0:FULL * P])
            sc.copy(gt_h[0:REST, FULL * P:], TB[0:REST, FULL * P:FC * P]).then_inc(s["gTh"], 1)

        def act_silu(sc, s, i, first=False):
            sc.wait_ge(s["G"], i + 1)
            if not first:
                sc.wait_ge(s["g"], i)
            sc.activation(act[:], GB[:, 0:F], ACT.Silu).then_inc(s["act"], 1)

        def act_rows(sc, s, i):
            sc.wait_ge(s["rt"], i + 1)
            sc.copy(rt_h[:], XB[:, 0:D]).then_inc(s["rth"], 1)

        def dve_gt(v, s, i):
            v.wait_ge(s["gTh"], i + 1)
            v.tensor_tensor(gt_l[:, 0:FULL * P], TB[:, 0:FULL * P], gt_h[:, 0:FULL * P].bitcast(F32), ALU.subtract)
            v.tensor_tensor(gt_l[0:REST, FULL * P:], TB[0:REST, FULL * P:FC * P],
                            gt_h[0:REST, FULL * P:].bitcast(F32), ALU.subtract).then_inc(s["gTl"], 1)

        def dve_g(v, s, i, first=False):
            v.wait_ge(s["act"], i + 1)
            v.wait_ge(s["U"], i + 1)
            if not first:
                v.wait_ge(s["gT"], i)
            v.tensor_tensor(g[:], UB[:, 0:F], act[:], ALU.mult).then_inc(s["g"], 1)

        def dve_rows(v, s, i):
            v.wait_ge(s["rth"], i + 1)
            v.tensor_tensor(rt_l[:], XB[:, 0:D], rt_h[:].bitcast(F32), ALU.subtract).then_inc(s["rtl"], 1)

        @block.tensor
        def _(pe):
            pe.wait_ge(s_ident, 1)
            pe.wait_ge(s_cw, 16 * 8)
            for k in range(K):
                for o in range(K):
                    pe.transpose(bank[k][:, o * P:(o + 1) * P], base_raw[:, o, k * P:(k + 1) * P], ident[:])
                pe.transpose(bank[k][:, D:D + ER], a_raw[:, k * P:(k + 1) * P], ident[:])
                pe.transpose(bank[2][:, k * P:(k + 1) * P], b_raw[:, k, :], ident[:])
                mm = pe.transpose(bank[3][:, k * E:(k + 1) * E], g_raw[:, k * P:(k + 1) * P], ident[0:E, 0:E])
            mm.then_inc(s_wt, 1)

            def turn_x(i, par):
                pe.wait_ge(s_xin[par], half_of(i, par) * 16 + 16)
                for k in range(K):
                    mm = pe.transpose(TX[:, k * P:(k + 1) * P], xin[par][:, k * P:(k + 1) * P], ident[:])
                mm.then_inc(s_tx, 1)

            def main(i, par, k):
                if k == 0:
                    pe.wait_ge(s_txh, i + 1)
                    pe.wait_ge(s_txl, i + 1)
                    if not (isinstance(i, int) and i < 4):
                        pe.wait_ge(s_x1, i - 3)
                mm = three_pass(pe, MAIN[par][:, 0:D + ER], xt_h[par % 2][:, k * P:(k + 1) * P],
                                xt_l[par % 2][:, k * P:(k + 1) * P], wa_h[:, k, :], wa_l[:, k, :],
                                k == 0, k == K - 1)
                if k == K - 1:
                    mm.then_inc(s_main, 1)

            def turn_hw(i):
                pe.wait_ge(s_hw, i + 1)
                pe.transpose(THW[:, 0:P], hw[:], ident[:]).then_inc(s_thw, 1)

            def lora_out(i, par):
                pe.wait_ge(s_hwh, i + 1)
                pe.wait_ge(s_hwl, i + 1)
                for a, b in ((hw_h, b_h), (hw_h, b_l), (hw_l, b_h)):
                    mm = pe.matmul(MAIN[par][:, 0:D], a[:], b[:], start=False, stop=a is hw_l,
                                   skip_group_check=True)
                mm.then_inc(s_p, 1)

            def turn_x1(i, par):
                pe.wait_ge(s_x1, i + 1)
                for k in range(K):
                    mm = pe.transpose(TX1[:, k * P:(k + 1) * P], x1[par][:, k * P:(k + 1) * P], ident[:])
                mm.then_inc(s_tx1, 1)

            def router(i, first=False):
                pe.wait_ge(s_x1t, i + 1)
                if not first:
                    pe.wait_ge(s_lgc, i)
                for k in range(K):
                    mm = pe.matmul(LG[:, 0:E], x1t[:, k * P:(k + 1) * P], gate_t[:, k, :],
                                   start=(k == 0), stop=(k == K - 1))
                mm.then_inc(s_lg, 1)

            def step(i, par):
                lo, hi = isinstance(i, int) and i < 2, isinstance(i, int)
                main(i, par, 0)
                if not (lo and i < 1):
                    turn_hw(i - 1)
                if not lo:
                    turn_x1(i - 2, par % 2)
                if not (hi and i + 1 >= NT):
                    turn_x(i + 1, 1 - par % 2)
                main(i, par, 1)
                if not (lo and i < 1):
                    lora_out(i - 1, (par - 1) % 4)
                if not lo:
                    router(i - 2, hi and i == 2)

            pe.wait_ge(s_wth, 1)
            pe.wait_ge(s_wtl, 1)
            turn_x(0, 0)
            for i in range(4):
                step(i, i)
            pairs(pe, 4, NT - 1, step, 4)
            step(NT - 1, (NT - 1) % 4)
            turn_hw(NT - 1)
            turn_x1(NT - 2, NT % 2)
            router(NT - 2)
            lora_out(NT - 1, (NT - 1) % 4)
            turn_x1(NT - 1, (NT - 1) % 2)
            router(NT - 1)

            pe.wait_ge(s_const, 1)
            pe.wait_ge(s_mark, 1)
            W = (NT + 1) * E
            pe.matmul(bank[6][:, 0:W], tri[:], mark[:].rearrange("p t e -> p (t e)"), start=True, stop=True)
            for t in range(NT):
                n = NT - t
                src = mark[:, t:t + 1, :].broadcast_to([P, n, E])
                mm = pe.matmul(bank[6][:, (t + 1) * E:W], ones[:], src, start=False, stop=(t == NT - 1),
                               skip_group_check=True)
            mm.then_inc(s_rank, 1)

            def perm_step(t, start, stop):
                pe.wait_ge(s_hot, t + 1)
                for c in range(TOPK):
                    mm = pe.matmul(bank[7][:, 0:NBLKP], row_hot[c][:], blk_hot[c][:],
                                   start=start and c == 0, stop=stop and c == TOPK - 1)
                mm.then_inc(s_permmm, 1)
            perm_step(0, True, False)
            with pe.Fori(1, NT - 1) as t:
                perm_step(t, False, False)
            perm_step(NT - 1, False, True)

            pe.wait_ge(s_routed, 1)
            pe.wait_ge(s_wdone, 6 * NE)

            def e_turn_rows(i, par):
                pe.wait_ge(s_rows[par], half_of(i, par) * 16 + 16)
                pe_turn_rows(pe, fe, rows[par])

            def load_e(i):
                return pe.value_load(blk_e[0:1, bass.ds(i, 1)], min_val=0, max_val=E - 1)

            def e_down(i):
                e = load_e(i)
                if not (isinstance(i, int) and i == 0):
                    pe.wait_ge(fe["y"], i)
                pe_down(pe, fe, i, e, True, True)

            def e_step(i, par):
                pe_turn_g(pe, fe, i - 1)
                pe_gate_up(pe, fe, load_e(i), i + 1)
                if not (isinstance(i, int) and i == NBLK - 1):
                    e_turn_rows(i + 1, 1 - par)
                e_down(i - 1)

            e_turn_rows(0, 0)
            pe_gate_up(pe, fe, load_e(0), 1)
            e_turn_rows(1, 1)
            e_step(1, 1)
            pairs(pe, 2, NBLK - 1, e_step)
            e_step(NBLK - 1, (NBLK - 1) % 2)
            pe_turn_g(pe, fe, NBLK - 1)
            e_down(NBLK - 1)

            def s_turn_rows(t, par):
                pe.wait_ge(s_srow[par], half_of(t, par) * 16 + 16)
                pe_turn_rows(pe, fs, rows[par])

            def s_step(t, par, first=False, last=False):
                if not first:
                    pe_turn_g(pe, fs, t * 2 - 1)
                pe_gate_up(pe, fs, E, t + 1)
                if not first:
                    pe_down(pe, fs, t * 2 - 1, E + 1, False, True)
                pe_turn_g(pe, fs, t * 2)
                pe_gate_up(pe, fs, E + 1, t + 1)
                if not last:
                    s_turn_rows(t + 1, 1 - par)
                if not first:
                    pe.wait_ge(fs["y"], t)
                pe_down(pe, fs, t * 2, E, True, False)

            pe.wait_ge(fe["y"], NBLK)
            s_turn_rows(0, 0)
            s_step(0, 0, first=True)
            pairs(pe, 1, NT - 1, s_step)
            s_step(NT - 1, (NT - 1) % 2, last=True)
            pe_turn_g(pe, fs, 2 * NT - 1)
            pe_down(pe, fs, 2 * NT - 1, E + 1, False, True)

        @block.scalar
        def _(sc):
            sc.wait_ge(s_ident, 1)
            sc.activation(logits[0:1, 0, 0:1], ident[0:1, 0:1], ACT.Silu).then_inc(s_warm, 1)
            sc.wait_ge(s_wt, 1)
            for k in range(K):
                sc.copy(wa_h[:, k, :], bank[k][:, 0:D + ER])
            sc.copy(b_h[:], bank[2][:, 0:D])
            sc.copy(gate_t[:].rearrange("p k e -> p (k e)"), bank[3][:, 0:K * E]).then_inc(s_wth, 1)

            def a_x(i, par):
                sc.wait_ge(s_tx, i + 1)
                if not (isinstance(i, int) and i < 2):
                    sc.wait_ge(s_main, i - 1)
                sc.copy(xt_h[par][:], TX[:, 0:D]).then_inc(s_txh, 1)

            def a_hw(i):
                sc.wait_ge(s_thw, i + 1)
                sc.copy(hw_h[:], THW[:, 0:P]).then_inc(s_hwh, 1)

            def a_x1(i):
                sc.wait_ge(s_tx1, i + 1)
                sc.copy(x1t[:], TX1[:, 0:D]).then_inc(s_x1t, 1)

            def step(i, par):
                if not (isinstance(i, int) and i < 1):
                    a_hw(i - 1)
                if not (isinstance(i, int) and i < 2):
                    a_x1(i - 2)
                if not (isinstance(i, int) and i + 1 >= NT):
                    a_x(i + 1, 1 - par)
            a_x(0, 0)
            for i in range(3):
                step(i, i % 2)
            pairs(sc, 3, NT - 1, step)
            step(NT - 1, (NT - 1) % 2)
            a_hw(NT - 1)
            a_x1(NT - 2)
            a_x1(NT - 1)

            sc.wait_ge(s_exp_in, 1)
            sc.activation(prob[:], tmp[:], ACT.Exp).then_inc(s_exp, 1)
            sc.wait_ge(s_routed, 1)
            sc.activation(act[0:1, 0:1], ident[0:1, 0:1], ACT.Silu)

            def e_y(i, par):
                sc.wait_ge(fe["D"], i + 1)
                if not (isinstance(i, int) and i < 2):
                    sc.wait_ge(s_yst[par], half_of(i, par) * 16)
                sc.copy(y_sb[par][:], YB[:, 0:D]).then_inc(fe["y"], 1)

            def e_step(i, par):
                act_gt(sc, fe, i - 1)
                act_silu(sc, fe, i)
                if not (isinstance(i, int) and i == NBLK - 1):
                    act_rows(sc, fe, i + 1)
                e_y(i - 1, 1 - par)
            act_rows(sc, fe, 0)
            act_silu(sc, fe, 0, True)
            act_rows(sc, fe, 1)
            for i in (1, 2):
                e_step(i, i % 2)
            pairs(sc, 3, NBLK - 1, e_step)
            e_step(NBLK - 1, (NBLK - 1) % 2)
            act_gt(sc, fe, NBLK - 1)
            e_y(NBLK - 1, (NBLK - 1) % 2)

            def s_step(t, par, first=False, last=False):
                if not first:
                    act_gt(sc, fs, t * 2 - 1)
                act_silu(sc, fs, t * 2, first)
                act_gt(sc, fs, t * 2)
                act_silu(sc, fs, t * 2 + 1)
                if not last:
                    act_rows(sc, fs, t + 1)
            act_rows(sc, fs, 0)
            s_step(0, 0, first=True)
            pairs(sc, 1, NT - 1, s_step)
            s_step(NT - 1, (NT - 1) % 2, last=True)
            act_gt(sc, fs, 2 * NT - 1)

        @block.vector
        def _(v):
            v.wait_ge(s_wth, 1)
            for k in range(K):
                v.tensor_tensor(wa_l[:, k, :], bank[k][:, 0:D + ER], wa_h[:, k, :].bitcast(F32), ALU.subtract)
            v.tensor_tensor(b_l[:], bank[2][:, 0:D], b_h[:].bitcast(F32), ALU.subtract).then_inc(s_wtl, 1)
            v.wait_ge(s_warm, 1)

            def v_x(i, par):
                v.wait_ge(s_txh, i + 1)
                v.tensor_tensor(xt_l[par][:], TX[:, 0:D], xt_h[par][:].bitcast(F32), ALU.subtract).then_inc(s_txl, 1)

            def v_hw(i, par):
                v.wait_ge(s_main, i + 1)
                w = w_tok[:, bass.ds(i, 1), :].rearrange("p t (e r) -> p (t e) r", r=1).broadcast_to([P, E, RANK])
                v.scalar_tensor_tensor(out=hw[:].rearrange("p (e r) -> p e r", e=E),
                                       in0=MAIN[par][:, D:D + ER].rearrange("p (e r) -> p e r", e=E),
                                       scalar=LORA_SCALING, in1=w, op0=ALU.mult, op1=ALU.mult).then_inc(s_hw, 1)

            def v_hwl(i):
                v.wait_ge(s_hwh, i + 1)
                v.tensor_tensor(hw_l[:], THW[:, 0:P], hw_h[:].bitcast(F32), ALU.subtract).then_inc(s_hwl, 1)

            def v_x1(i, par):
                v.wait_ge(s_p, i + 1)
                if not (isinstance(i, int) and i < 2):
                    v.wait_ge(s_x1st[par % 2], half_of(i, par) * 16)
                v.tensor_tensor(x1[par % 2][:], MAIN[par][:, 0:D], bias[:], ALU.add).then_inc(s_x1, 1)

            def v_lg(i):
                v.wait_ge(s_lg, i + 1)
                v.tensor_copy(logits[:, bass.ds(i, 1), :].rearrange("p t e -> p (t e)"), LG[:, 0:E]).then_inc(s_lgc, 1)

            def step(i, par):
                if not (isinstance(i, int) and i < 1):
                    v_hwl(i - 1)
                if not (isinstance(i, int) and i + 1 >= NT):
                    v_x(i + 1, 1 - par % 2)
                v_hw(i, par)
                if not (isinstance(i, int) and i < 1):
                    v_x1(i - 1, (par - 1) % 4)
                if not (isinstance(i, int) and i < 2):
                    v_lg(i - 2)
            v_x(0, 0)
            for i in range(4):
                step(i, i)
            pairs(v, 4, NT - 1, step, 4)
            step(NT - 1, (NT - 1) % 4)
            v_hwl(NT - 1)
            v_lg(NT - 2)
            v_x1(NT - 1, (NT - 1) % 4)
            v_lg(NT - 1)

            count = [0]

            def link(ins):
                count[0] += 1
                ins.then_inc(s_r, 1)
                v.wait_ge(s_r, count[0])

            def over_e(a):
                return a[:].rearrange("p (t o) -> p t o", o=1).broadcast_to([P, NT, E])

            v.wait_ge(s_const, 1)
            v.wait_ge(s_lgc, NT)
            link(v.tensor_reduce(red[:], logits[:], AX.X, ALU.max))
            v.tensor_tensor(tmp[:], logits[:], over_e(red), ALU.subtract).then_inc(s_exp_in, 1)
            v.wait_ge(s_exp, 1)
            link(v.tensor_reduce(red[:], prob[:], AX.X, ALU.add))
            link(v.reciprocal(red[:], red[:]))
            link(v.tensor_tensor(prob[:], prob[:], over_e(red), ALU.mult))
            for c, p in enumerate((prob, prob2)):
                link(v.tensor_reduce(top_v[c][:], p[:], AX.X, ALU.max))
                link(v.tensor_tensor(tmp[:], p[:], over_e(top_v[c]), ALU.is_equal))
                link(v.tensor_tensor(tmp[:], tmp[:],
                                     down_e[:].rearrange("p (o e) -> p o e", o=1).broadcast_to([P, NT, E]), ALU.mult))
                link(v.tensor_reduce(red[:], tmp[:], AX.X, ALU.max))
                link(v.tensor_tensor(hot[c][:], tmp[:], over_e(red), ALU.is_equal))
                if c == 0:
                    link(v.scalar_tensor_tensor(out=prob2[:].rearrange("p t e -> p (t e)"),
                                                in0=hot[0][:].rearrange("p t e -> p (t e)"), scalar=-2.0,
                                                in1=prob[:].rearrange("p t e -> p (t e)"),
                                                op0=ALU.mult, op1=ALU.add))
            v.tensor_tensor(mark[:, 0:NT, :], hot[0][:], hot[1][:], ALU.add).then_inc(s_mark, 1)
            link(v.tensor_tensor(red[:], top_v[0][:], top_v[1][:], ALU.add))
            link(v.tensor_scalar(red[:], red[:], 1e-20, None, ALU.add))
            link(v.reciprocal(red[:], red[:]))
            for c in range(TOPK):
                link(v.tensor_tensor(top_w[c][:], top_v[c][:], red[:], ALU.mult))
                link(v.tensor_scalar(top_w[c][:], top_w[c][:], ROUTED_SCALE, None, ALU.mult))
            v.wait_ge(s_rank, 1)
            total = bank[6][:, NT * E:(NT + 1) * E]
            link(v.tensor_copy(nb[:], total))
            link(v.tensor_tensor(over[:], nb[:].rearrange("p (e o) -> p e o", o=1).broadcast_to([P, E, NT]),
                                 step128[:].rearrange("p (o t) -> p o t", o=1).broadcast_to([P, E, NT]), ALU.is_gt))
            link(v.tensor_reduce(nb[:], over[:], AX.X, ALU.add))
            link(v.tensor_tensor(ee[:], upto[:],
                                 nb[:].rearrange("p (o e) -> p o e", o=1).broadcast_to([P, E, E]), ALU.mult))
            link(v.tensor_reduce(bend[:], ee[:], AX.X, ALU.add))
            link(v.tensor_tensor(bbase[:], bend[:], nb[:], ALU.subtract))
            link(v.tensor_scalar(bbase[:], bbase[:], float(P), None, ALU.mult))
            link(v.tensor_tensor(pos[:], bank[6][:, 0:NT * E].rearrange("p (t e) -> p t e", e=E),
                                 bbase[:].rearrange("p (o e) -> p o e", o=1).broadcast_to([P, NT, E]), ALU.add))
            for c in range(TOPK):
                link(v.tensor_tensor(tmp[:], pos[:], hot[c][:], ALU.mult))
                link(v.tensor_reduce(slot_f[:, c, :], tmp[:], AX.X, ALU.add))
            link(v.tensor_copy(slot_i[:], slot_f[:]))
            link(v.tensor_scalar(part_i[:], slot_i[:], 7, None, ALU.logical_shift_right))
            link(v.tensor_copy(blk_of[:], part_i[:]))
            link(v.tensor_scalar(part_i[:], slot_i[:], P - 1, None, ALU.bitwise_and))
            link(v.tensor_copy(row_of[:], part_i[:]))
            link(v.tensor_tensor(blk_cmp[:],
                                 iota_blk[0:1, :].rearrange("p (b o) -> p b o", o=1).broadcast_to([1, NBLKP, E]),
                                 bend[0:1, :].rearrange("p (o e) -> p o e", o=1).broadcast_to([1, NBLKP, E]), ALU.is_ge))
            link(v.tensor_reduce(blk_ef[:], blk_cmp[:], AX.X, ALU.add))
            link(v.tensor_scalar(blk_ef[:], blk_ef[:], float(E - 1), None, ALU.min))
            link(v.tensor_copy(blk_e[:], blk_ef[:]))

            def hots(t, first=False):
                if not first:
                    v.wait_ge(s_permmm, t)
                for c in range(TOPK):
                    v.tensor_scalar(row_hot[c][:], iota_row[:], row_of[:, c, bass.ds(t, 1)], None, ALU.is_equal)
                    ins = v.tensor_scalar(blk_hot[c][:], iota_blk[:], blk_of[:, c, bass.ds(t, 1)],
                                          tok_id[:, bass.ds(t, 1)], ALU.is_equal, ALU.mult)
                ins.then_inc(s_hot, 1)
            hots(0, True)
            with v.Fori(1, NT) as t:
                hots(t)
            v.wait_ge(s_permmm, NT)
            v.tensor_copy(perm_i[:], bank[7][:, 0:NBLKP]).then_inc(s_routed, 1)

            def e_step(i, par):
                dve_gt(v, fe, i - 1)
                dve_g(v, fe, i)
                if not (isinstance(i, int) and i == NBLK - 1):
                    dve_rows(v, fe, i + 1)
            dve_rows(v, fe, 0)
            dve_g(v, fe, 0, True)
            dve_rows(v, fe, 1)
            e_step(1, 1)
            pairs(v, 2, NBLK - 1, e_step)
            e_step(NBLK - 1, (NBLK - 1) % 2)
            dve_gt(v, fe, NBLK - 1)

            def mix(t, par):
                v.wait_ge(s_res[par], half_of(t, par) * 16 + 16)
                v.wait_ge(s_pick[par], half_of(t, par) * 32 + 32)
                for c in range(TOPK):
                    v.scalar_tensor_tensor(out=res[par][:], in0=pick[c][par][:], scalar=top_w[c][:, bass.ds(t, 1)],
                                           in1=res[par][:], op0=ALU.mult, op1=ALU.add).then_inc(s_mix, 1)
                    v.wait_ge(s_mix, t * 2 + (c + 1))

            def final(t, par, first=False):
                v.wait_ge(fs["D"], t * 2 + 2)
                if not first:
                    v.wait_ge(s_out[par], half_of(t, par) * 16)
                v.tensor_tensor(y_sb[par][:], YB[:, 0:D], res[par][:], ALU.add).then_inc(fs["y"], 1)

            def s_step(t, par, first=False, last=False):
                if not first:
                    dve_gt(v, fs, t * 2 - 1)
                dve_g(v, fs, t * 2, first)
                if not first:
                    final(t - 1, 1 - par, isinstance(t, int) and t < 3)
                dve_gt(v, fs, t * 2)
                dve_g(v, fs, t * 2 + 1)
                if not last:
                    dve_rows(v, fs, t + 1)
                mix(t, par)
            dve_rows(v, fs, 0)
            s_step(0, 0, first=True)
            for t in (1, 2):
                s_step(t, t % 2)
            pairs(v, 3, NT - 1, s_step)
            s_step(NT - 1, (NT - 1) % 2, last=True)
            dve_gt(v, fs, 2 * NT - 1)
            final(NT - 1, (NT - 1) % 2)


_INS = ['x', 'cond_8', 'L0_cond_W_base', 'L0_cond_b_base', 'L0_cond_As', 'L0_cond_Bs', 'L0_ffn_gate_w',
        'L0_ffn_w_gate', 'L0_ffn_w_up', 'L0_ffn_w_down', 'L0_ffn_sw_gate', 'L0_ffn_sw_up', 'L0_ffn_sw_down']


def kernel(**inputs):
    import numpy as _np
    import concourse.bacc as _bacc
    from concourse import mybir as _mybir
    from concourse.bass_utils import run_bass_kernel_spmd as _run

    nc = _bacc.Bacc("TRN2", target_bir_lowering=False, num_devices=1)
    arrays, args = {}, []
    for name in _INS:
        a = _np.ascontiguousarray(inputs[name])
        arrays[f"in_{name}_dram"] = a
        args.append(nc.dram_tensor(f"in_{name}_dram", a.shape, _mybir.dt.from_np(a.dtype), kind="ExternalInput").ap())
    args.append(nc.dram_tensor("out_0_dram", inputs['x'].shape, _mybir.dt.float32, kind="ExternalOutput").ap())
    adaln_moe(nc, *args)
    r = _run(nc, [arrays], core_ids=[0])
    return r.results[0]["out_0_dram"]
```

```python
from contextlib import ExitStack

import concourse.bass as bass
from concourse import mybir

F32 = mybir.dt.float32
F32R = mybir.dt.float32r
BF16 = mybir.dt.bfloat16
I32 = mybir.dt.int32
U32 = mybir.dt.uint32
ALU = mybir.AluOpType
ACT = mybir.ActivationFunctionType
AX = mybir.AxisListType

P = 128
TOPK = 2
LORA_SCALING = 2.0
ROUTED_SCALE = 2.5


def adaln_moe(nc, x, cond, w_base, b_base, lora_a, lora_b, gate_w, w_gate, w_up, w_down,
              sw_gate, sw_up, sw_down, out):
    NB, SEQ, D = x.shape
    E, RANK, _ = lora_a.shape
    F = w_gate.shape[2]
    T = NB * SEQ
    NT = T // P
    K = D // P
    ER = E * RANK
    NS = sw_gate.shape[1] // F
    NE = E + NS
    FULL = F // P
    REST = F - FULL * P
    FC = FULL + 1
    NBLK = (TOPK * T + E * (P - 1)) // P
    NBLKP = NBLK + NBLK % 2
    DX = D + E
    HOT0 = 4
    HOT1 = HOT0 + NT // 4
    NPRE = HOT1 + 2
    FIN_A = 3 * NPRE - NT + 2
    RANK_AT = 2
    MATH = 6
    assert HOT1 % 2 == 0 and NPRE % 2 == 0 and FIN_A % 2 == 0 and FIN_A >= 2 and NPRE > FIN_A
    assert SEQ * 2 == P and K == 2 and ER == P and NS == 2 and E == 8 and REST > 0

    x_rows = x.rearrange("b s d -> (b s) d")
    out_rows = out.rearrange("b s d -> (b s) d")
    x1_dram = nc.dram_tensor("x1_rows", (T, D), F32, kind="Internal").ap()
    y_dram = nc.dram_tensor("y_slots", (NBLK * P, D), F32, kind="Internal").ap()

    base_dram = nc.dram_tensor("base_rows", (NPRE * P, D), F32, kind="Internal").ap()

    with ExitStack() as ctx:
        def sb(name, shape, dt=F32, where=ctx):
            return where.enter_context(nc.sbuf_tensor(name, shape, dt))

        def sem(name):
            return ctx.enter_context(nc.semaphore(name))

        bank = [ctx.enter_context(nc.psum_tensor(f"bank{i}", [P, 512], F32)) for i in range(8)]

        gu_h = sb("gu_h", [P, NE, K, 2 * F], F32R)
        dn_h = sb("dn_h", [P, NE, FC, D], F32R)
        with ExitStack() as own:
            gu_own = sb("gu_own", [P, NE, K, 2 * F], F32, own)
            dn_own = sb("dn_own", [P, NE, FC, D], F32, own)
        gu_l = sb("gu_l", [P, NE, K, 2 * F], F32R)
        dn_l = sb("dn_l", [P, NE, FC, D], F32R)
        ident = sb("ident", [P, P])
        spare = sb("spare", [1, 4])
        logits = sb("logits", [P, NT, E])
        top_w = [sb(f"top_w{c}", [P, NT]) for c in range(TOPK)]
        slot_i = sb("slot_i", [P, TOPK, NT], I32)
        perm_i = sb("perm_i", [P, NBLKP], I32)
        blk_e = sb("blk_e", [1, NBLKP], I32)
        blk_pack = sb("blk_pack", [1, NBLKP], I32)
        rows = [sb(f"rows{i}", [P, D]) for i in range(2)]
        rt_h = sb("rt_h", [P, D], F32R)
        rt_l = sb("rt_l", [P, D], F32R)
        act = sb("act", [P, F])
        g = sb("g", [P, FC * P])
        down_e = sb("down_e", [P, E])
        tri = sb("tri", [P, P], BF16)
        ones = sb("ones", [P, P], BF16)
        step128 = sb("step128", [P, NT])
        upto = sb("upto", [P, E, E])
        iota_row = sb("iota_row", [P, P])
        iota_blk = sb("iota_blk", [P, NBLKP])
        tok_id = sb("tok_id", [P, NT])
        mark = sb("mark", [P, NT + 1, E], BF16)

        with ExitStack() as proj:
            wa_h = sb("wa_h", [P, K, DX + ER], F32R, proj)
            wa_l = sb("wa_l", [P, K, DX + ER], F32R, proj)
            b_h = sb("b_h", [P, DX], F32R, proj)
            b_l = sb("b_l", [P, DX], F32R, proj)
            bias = sb("bias", [P, DX], F32, proj)
            w_tok = sb("w_tok", [P, NT, E], F32, proj)
            xin = [sb(f"xin{i}", [P, 2, D], F32, proj) for i in range(2)]
            hw = sb("hw", [P, ER], F32, proj)
            hw_h = sb("hw_h", [P, P], F32R, proj)
            hw_l = sb("hw_l", [P, P], F32R, proj)
            with ExitStack() as raw:
                base_raw = sb("base_raw", [P, K, D], F32, raw)
                a_raw = sb("a_raw", [P, D], F32, raw)
                b_raw = sb("b_raw", [P, K, ER], F32, raw)
                g_raw = sb("g_raw", [E, D], F32, raw)
                gate_t = sb("gate_t", [P, K, E], F32, raw)
                b_col = sb("b_col", [P, K], F32, raw)
            xt_h = [sb(f"xt_h{i}", [P, D], F32R, proj) for i in range(2)]
            xt_l = [sb(f"xt_l{i}", [P, D], F32R, proj) for i in range(2)]
            x1 = [sb(f"x1_{i}", [P, 2, D], F32, proj) for i in range(2)]
        with ExitStack() as ffn:
            gt_h = sb("gt_h", [P, FC * P], F32R, ffn)
            gt_l = sb("gt_l", [P, FC * P], F32R, ffn)
            y_sb = [sb(f"y_sb{i}", [P, D], F32, ffn) for i in range(2)]
            res = [sb(f"res{i}", [P, D], F32, ffn) for i in range(2)]
            with ExitStack() as route:
                R3 = [P, NT, E]
                with ExitStack() as math:
                    prob = sb("prob", R3, F32, math)
                    prob2 = sb("prob2", R3, F32, math)
                    pos = sb("pos", R3, F32, math)
                    tmp = sb("tmp", R3, BF16, math)
                    hot = [sb(f"hot{c}", R3, BF16, math) for c in range(TOPK)]
                    over = sb("over", [P, E, NT], BF16, math)
                row_hot = [[sb(f"row_hot{c}_{i}", [P, P], F32R, route) for i in range(4)] for c in range(TOPK)]
                blk_hot = [[sb(f"blk_hot{c}_{i}", [P, NBLKP], F32R, route) for i in range(4)] for c in range(TOPK)]
                red = sb("red", [P, NT], F32, route)
                top_v = [sb(f"top_v{c}", [P, NT], F32, route) for c in range(TOPK)]
                ee = sb("ee", [P, E, E], F32, route)
                nb = sb("nb", [P, E], F32, route)
                bend = sb("bend", [P, E], F32, route)
                bbase = sb("bbase", [P, E], F32, route)
                slot_f = sb("slot_f", [P, TOPK, NT], F32, route)
                part_i = sb("part_i", [P, TOPK, NT], I32, route)
                blk_of = sb("blk_of", [P, TOPK, NT], F32, route)
                row_of = sb("row_of", [P, TOPK, NT], F32, route)
                blk_cmp = sb("blk_cmp", [1, NBLKP, E], BF16, route)
                blk_ef = sb("blk_ef", [1, NBLKP], F32, route)
                pack_f = sb("pack_f", [1, NBLKP], F32, route)
            idx = [sb(f"idx{i}", [P, 1], I32, ffn) for i in range(2)]
            pick = [[sb(f"pick{c}_{i}", [P, D], F32, ffn) for i in range(2)] for c in range(TOPK)]
            pidx = [[sb(f"pidx{c}_{i}", [P, 1], I32, ffn) for i in range(2)] for c in range(TOPK)]
            e_res = [sb(f"e_res{i}", [P, D], F32, ffn) for i in range(2)]
            e_pick = [[sb(f"e_pick{c}_{i}", [P, D], F32, ffn) for i in range(2)] for c in range(TOPK)]
            e_pidx = [[sb(f"e_pidx{c}_{i}", [P, 1], I32, ffn) for i in range(2)] for c in range(TOPK)]

        s_ident = sem("s_ident")
        s_const = sem("s_const")
        s_cw = sem("s_cw")
        s_cwt, s_gate, s_cwf = sem("s_cwt"), sem("s_gate"), sem("s_cwf")
        s_cwh, s_cwl = sem("s_cwh"), sem("s_cwl")
        s_raw = [sem(f"s_raw{u}") for u in range(2)]
        s_whi, s_wlo = sem("s_whi"), sem("s_wlo")
        s_pool = sem("s_pool")

        s_xin = [sem(f"s_xin{i}") for i in range(2)]
        s_tx, s_txh, s_txl = sem("s_tx"), sem("s_txh"), sem("s_txl")
        s_main, s_hw, s_thw = sem("s_main"), sem("s_hw"), sem("s_thw")
        s_hwh, s_hwl = sem("s_hwh"), sem("s_hwl")
        s_p, s_x1, s_lg = sem("s_p"), sem("s_x1"), sem("s_lg")
        s_x1st = [sem(f"s_x1st{i}") for i in range(2)]

        s_r, s_exp, s_exp_in, s_gz = sem("s_r"), sem("s_exp"), sem("s_exp_in"), sem("s_gz")
        s_mark, s_rank = sem("s_mark"), sem("s_rank")
        s_hot = sem("s_hot")
        s_perm, s_routed = sem("s_perm"), sem("s_routed")

        def ffn_sems(tag):
            names = "row rt rth rtl G U act g gT gTh gTl D y".split()
            return {n: [sem(f"{tag}_{n}{i}") for i in range(2)] if n == "row" else sem(f"{tag}_{n}")
                    for n in names}

        fp, fe, fs = ffn_sems("pre"), ffn_sems("ex"), ffn_sems("post")
        s_yst = [sem(f"s_yst{i}") for i in range(2)]
        s_idx = sem("s_idx")
        s_bres = [sem(f"s_bres{i}") for i in range(2)]
        s_bout = [sem(f"s_bout{i}") for i in range(2)]
        s_res = [sem(f"s_res{i}") for i in range(2)]
        s_pick = [sem(f"s_pick{i}") for i in range(2)]
        s_pidx, s_mix = sem("s_pidx"), sem("s_mix")
        s_out = [sem(f"s_out{i}") for i in range(2)]
        s_epidx, s_emix = sem("s_epidx"), sem("s_emix")
        s_eres, s_epick, s_eout = ([sem(f"s_e{n}{i}") for i in range(2)] for n in "res pick out".split())

        block = ctx.enter_context(nc.Block())

        TX, MAIN, THW = bank[0], bank[1:5], bank[5]
        XB, GB, UB, TB, YB, RANK_B, PERM_B = bank[0], bank[1], bank[2], bank[3], bank[4], bank[6], bank[7]

        def known(i, below):
            return isinstance(i, int) and i < below

        def three_pass(pe, o, lh, ll, rh, rl, start, stop, skip=False):
            pe.matmul(o, lh, rh, start=start, stop=False, skip_group_check=skip)
            pe.matmul(o, lh, rl, start=False, stop=False, skip_group_check=skip)
            return pe.matmul(o, ll, rh, start=False, stop=stop, skip_group_check=skip)

        def turns(eng, lo, hi, step, n=2, after=None):
            count = (hi - lo) // n
            if count:
                with eng.Fori(0, count) as j:
                    for u in range(n):
                        step(j * n + (lo + u), (lo + u) % n)
                        if after:
                            after(j, u)
            for i in range(lo + n * count, hi):
                step(i, i % n)

        def with_early(eng, step):
            def one(m, par):
                step(m, par, m, par)
            one(0, 0)
            one(1, 1)
            turns(eng, 2, FIN_A, one)
            with eng.Fori(0, (NPRE - FIN_A) // 2) as j:
                for d in range(2):
                    step(j * 4 + (FIN_A + 2 * d), 0, j * 2 + (FIN_A + d), d)
                    step(j * 4 + (FIN_A + 2 * d + 1), 1, None, None)

        def half_of(i, par):
            return i // 2 if isinstance(i, int) else (i - par % 2) // 2

        def quarter_of(i, par):
            return i // 4 if isinstance(i, int) else (i - par) // 4

        def weight_parts(e):
            for k in range(K):
                yield tuple(w[:, bass.ds(e, 1), k, :].rearrange("p e f -> p (e f)") for w in (gu_own, gu_h, gu_l))
            yield tuple(w[:, bass.ds(e, 1), 0:FULL, :].rearrange("p e c d -> p (e c d)") for w in (dn_own, dn_h, dn_l))
            yield tuple(w[0:REST, bass.ds(e, 1), FULL, :].rearrange("p e d -> p (e d)") for w in (dn_own, dn_h, dn_l))

        def hots(v, t, buf):
            if not known(t, 4):
                v.wait_ge(s_perm, t - 3)
            for c in range(TOPK):
                v.tensor_scalar(row_hot[c][buf][:], iota_row[:], row_of[:, c, bass.ds(t, 1)], None, ALU.is_equal)
                ins = v.tensor_scalar(blk_hot[c][buf][:], iota_blk[:], blk_of[:, c, bass.ds(t, 1)],
                                      tok_id[:, bass.ds(t, 1)], ALU.is_equal, ALU.mult)
            ins.then_inc(s_hot, 1)

        @block.sync
        def _(sp):
            sp.dma_start(g_raw[:], gate_w).then_inc(s_cw, 16)
            sp.dma_start(base_raw[:], w_base.rearrange("(k p) c -> p k c", p=P)).then_inc(s_cw, 16)
            sp.dma_start(a_raw[:], lora_a.rearrange("e r c -> (e r) c")).then_inc(s_cw, 16)
            for k in range(K):
                sp.dma_start(b_raw[:, k, :].rearrange("p (e r) -> p e r", e=E),
                             lora_b[:, k * P:(k + 1) * P, :].rearrange("e o r -> o e r")).then_inc(s_cw, 16)
            sp.dma_start(bias[:, 0:D], b_base.rearrange("(a o) -> a o", a=1).broadcast_to([P, D])).then_inc(s_cw, 16)
            for k in range(K):
                sp.dma_start(b_col[:, k:k + 1], b_base[k * P:(k + 1) * P].rearrange("(p a) -> p a", a=1)
                             ).then_inc(s_cw, 16)
            for h in range(2):
                sp.dma_start(w_tok[h * SEQ:(h + 1) * SEQ, :, :],
                             cond.rearrange("(a t h) e -> h a t e", a=1, h=2)[h].broadcast_to([SEQ, NT, E])
                             ).then_inc(s_cw, 16)

            def load_x(q, buf):
                if not known(q, 2):
                    sp.wait_ge(s_tx, q * 2 - 2)
                sp.dma_start(xin[buf][:], x_rows[bass.ds(q * (2 * P), 2 * P), :].rearrange("(t p) d -> p t d", p=P)
                             ).then_inc(s_xin[buf], 16)

            def store_x1(q, buf):
                sp.wait_ge(s_x1, q * 2 + 2)
                sp.dma_start(x1_dram[bass.ds(q * (2 * P), 2 * P), :].rearrange("(t p) d -> p t d", p=P),
                             x1[buf][:]).then_inc(s_x1st[buf], 16)

            def step_a(q, buf):
                load_x(q, buf)
                store_x1(q - 2, buf)
            load_x(0, 0)
            load_x(1, 1)
            turns(sp, 2, NT // 2, step_a)
            store_x1(NT // 2 - 2, 0)

            def load_rows(s, t, par, first):
                if not known(t, first + 2):
                    sp.wait_ge(s["rt"], t - (first + 1))
                sp.dma_start(rows[par][:], x1_dram[bass.ds(t * P, P), :]).then_inc(s["row"][par], 16)

            def load_res(t, par, done):
                sp.dma_start(res[par][:], x_rows[bass.ds(t * P, P), :]).then_inc(done[par], 16)

            def store_base(t, par):
                sp.wait_ge(fp["y"], t + 1)
                sp.dma_start(base_dram[bass.ds(t * P, P), :], y_sb[par][:]).then_inc(s_bout[par], 16)

            sp.wait_ge(s_x1st[0], 16)
            for t in range(2):
                load_rows(fp, t, t, 0)
            store_x1(NT // 2 - 1, 1)
            for p in range(2):
                sp.wait_ge(s_x1st[p], 16 * (NT // 4))
            for t in range(2):
                load_res(t, t, s_bres)

            def step_p(t, par):
                load_rows(fp, t, par, 0)
                store_base(t - 2, par)
                load_res(t, par, s_bres)
            turns(sp, 2, NPRE, step_p)
            store_base(NPRE - 2, NPRE % 2)
            store_base(NPRE - 1, (NPRE - 1) % 2)

            def store_y(i, par):
                sp.wait_ge(fe["y"], i + 1)
                sp.dma_start(y_dram[bass.ds(i * P, P), :], y_sb[par][:]).then_inc(s_yst[par], 16)
            turns(sp, 0, NBLK - 1, store_y)

            def store_out(u, par, ready):
                sp.wait_ge(*ready)
                sp.dma_start(out_rows[bass.ds((u + NPRE) * P, P), :], y_sb[par][:]).then_inc(s_out[par], 16)

            def store_early(q, par):
                sp.wait_ge(s_emix, q * 2 + 2)
                sp.dma_start(out_rows[bass.ds(q * P, P), :], e_res[par][:]).then_inc(s_eout[par], 16)

            def load_base(q, par):
                if not known(q, 2):
                    sp.wait_ge(s_eout[par], half_of(q, par) * 16)
                sp.dma_start(e_res[par][:], base_dram[bass.ds(q * P, P), :]).then_inc(s_eres[par], 16)

            sp.wait_ge(fe["rt"], NBLK)
            for t in range(NPRE, NPRE + 2):
                load_rows(fs, t, t % 2, NPRE)
                load_res(t, t % 2, s_res)
            store_y(NBLK - 1, (NBLK - 1) % 2)
            for i in range(2):
                sp.wait_ge(s_bout[i], 16 * (NPRE // 2))

            def step_s(m, par, q, q_par):
                load_rows(fs, m + (NPRE + 2), par, NPRE)
                sp.wait_ge(fs["y"], m + 1)
                load_res(m + (NPRE + 2), par, s_res)
                if q is not None:
                    load_base(q, q_par)
                store_out(m, par, (s_mix, m * 2 + 2))
                if q is not None:
                    store_early(q, q_par)
            with_early(sp, step_s)
            n = NT - NPRE
            store_out(n - 2, n % 2, (s_mix, 2 * n - 2))
            store_out(n - 1, (n - 1) % 2, (fs["y"], n))
            for i in range(2):
                sp.wait_ge(s_out[i], 16 * (n // 2))
                sp.wait_ge(s_eout[i], 16 * (NPRE // 2))

        @block.gpsimd
        def _(pool):
            n_pool = [0]

            def link(ins):
                n_pool[0] += 1
                ins.then_inc(s_pool, 1)
                pool.wait_ge(s_pool, n_pool[0])

            def before_dma():
                pool.tensor_tensor(spare[0:1, 1:2], spare[0:1, 0:1], spare[0:1, 0:1], ALU.add)

            link(pool.memset(spare[:], 0.0))
            link(pool.memset(ident[:], 1.0))
            pool.affine_select(out=ident[:], in_=ident[:], compare_op=ALU.is_equal, fill=0.0, base=0,
                               pattern=[[-1, P]], channel_multiplier=1).then_inc(s_ident, 1)

            small = dict(allow_small_or_imprecise_dtypes=True)
            pool.memset(g[:, F:], 0.0).then_inc(s_gz, 1)
            pool.iota(down_e[:], pattern=[[-1, E]], base=E, channel_multiplier=0, **small)
            pool.iota(step128[:], pattern=[[P, NT]], base=0, channel_multiplier=0, **small)
            pool.iota(iota_row[:], pattern=[[1, P]], base=0, channel_multiplier=0, **small)
            pool.iota(iota_blk[:], pattern=[[1, NBLKP]], base=0, channel_multiplier=0, **small)
            pool.iota(tok_id[:], pattern=[[P, NT]], base=0, channel_multiplier=1, **small)
            pool.memset(ones[:], 1.0)
            link(pool.memset(tri[:], 1.0))
            link(pool.affine_select(out=tri[:], in_=tri[:], compare_op=ALU.is_gt, fill=0.0, base=0,
                                    pattern=[[1, P]], channel_multiplier=-1))
            link(pool.memset(upto[:], 1.0))
            link(pool.affine_select(out=upto[:], in_=upto[:], compare_op=ALU.is_ge, fill=0.0, base=0,
                                    pattern=[[1, E], [-1, E]], channel_multiplier=0))
            pool.memset(mark[:, NT, :], 0.0).then_inc(s_const, 1)

            def low_parts(n):
                for part, (own_ap, hi, lo) in enumerate(weight_parts(n)):
                    pool.wait_ge(s_whi, n * 4 + part + 1)
                    pool.tensor_tensor(lo, own_ap, hi.bitcast(F32), ALU.subtract).then_inc(s_wlo, 1)

            for n in range(NS):
                low_parts(n)
            with pool.Fori(NS, NE) as n:
                low_parts(n)

            pool.wait_ge(s_routed, 1)
            pool.wait_ge(fp["rt"], NPRE)

            def gather(i, par):
                if not known(i, 2):
                    pool.wait_ge(fe["rt"], i - 1)
                pool.tensor_copy(idx[par][:], perm_i[:, bass.ds(i, 1)]).then_inc(s_idx, 1)
                pool.wait_ge(s_idx, i + 1)
                before_dma()
                pool.indirect_dma_start(rows[par][:], None, x1_dram,
                                        bass.IndirectOffsetOnAxis(ap=idx[par][:, 0:1], axis=0)
                                        ).then_inc(fe["row"][par], 16)
            gather(0, 0)
            gather(1, 1)
            turns(pool, 2, NBLK, gather)

            pool.wait_ge(s_yst[0], 16 * ((NBLK + 1) // 2))
            pool.wait_ge(s_yst[1], 16 * (NBLK // 2))

            def gather_y(t, count, to, to_idx, counted, landed):
                for c in range(TOPK):
                    pool.tensor_copy(to_idx[c][:], slot_i[:, c, bass.ds(t, 1)]).then_inc(counted, 1)
                    pool.wait_ge(counted, count + (c + 1))
                    before_dma()
                    pool.indirect_dma_start(to[c][:], None, y_dram,
                                            bass.IndirectOffsetOnAxis(ap=to_idx[c][:, 0:1], axis=0)
                                            ).then_inc(landed, 16)

            def gather_late(t, par):
                if not known(t, NPRE + 2):
                    pool.wait_ge(s_mix, (t - (NPRE + 1)) * 2)
                gather_y(t, (t - NPRE) * 2, [pick[c][par] for c in range(TOPK)],
                         [pidx[c][par] for c in range(TOPK)], s_pidx, s_pick[par])

            def gather_early(q, par):
                if not known(q, 2):
                    pool.wait_ge(s_emix, q * 2 - 2)
                gather_y(q, q * 2, [pick[par] for pick in e_pick], [pi[par] for pi in e_pidx], s_epidx, s_epick[par])

            def step_y(m, par, q, q_par):
                if q is not None:
                    gather_early(q, q_par)
                gather_late(m + (NPRE + 2), par)
            gather_late(NPRE, 0)
            gather_late(NPRE + 1, 1)
            with_early(pool, step_y)

        def pe_turn_g(pe, s, i):
            pe.wait_ge(s["g"], i + 1)
            for c in range(FC):
                mm = pe.transpose(TB[:, c * P:(c + 1) * P], g[:, c * P:(c + 1) * P], ident[:])
            mm.then_inc(s["gT"], 1)

        def pe_gate_up(pe, s, e, rows_ready):
            pe.wait_ge(s["rth"], rows_ready)
            pe.wait_ge(s["rtl"], rows_ready)
            for b, c, name in ((GB, 0, "G"), (UB, F, "U")):
                for k in range(K):
                    wh = gu_h[:, bass.ds(e, 1), k, c:c + F].rearrange("p e f -> p (e f)")
                    wl = gu_l[:, bass.ds(e, 1), k, c:c + F].rearrange("p e f -> p (e f)")
                    mm = three_pass(pe, b[:, 0:F], rt_h[:, k * P:(k + 1) * P], rt_l[:, k * P:(k + 1) * P],
                                    wh, wl, k == 0, k == K - 1)
                mm.then_inc(s[name], 1)

        def pe_turn_rows(pe, s, i, par):
            pe.wait_ge(s["row"][par], half_of(i, par) * 16 + 16)
            for k in range(K):
                mm = pe.transpose(XB[:, k * P:(k + 1) * P], rows[par][:, k * P:(k + 1) * P], ident[:])
            mm.then_inc(s["rt"], 1)

        def pe_down(pe, s, i, e, start, stop):
            pe.wait_ge(s["gTh"], i + 1)
            pe.wait_ge(s["gTl"], i + 1)
            for c in range(FC):
                n = P if c < FULL else REST
                wh = dn_h[0:n, bass.ds(e, 1), c, :].rearrange("p e d -> p (e d)")
                wl = dn_l[0:n, bass.ds(e, 1), c, :].rearrange("p e d -> p (e d)")
                mm = three_pass(pe, YB[:, 0:D], gt_h[0:n, c * P:(c + 1) * P], gt_l[0:n, c * P:(c + 1) * P],
                                wh, wl, start and c == 0, stop and c == FC - 1)
            mm.then_inc(s["D"], 1)

        def act_gt(sc, s, i):
            sc.wait_ge(s["gT"], i + 1)
            sc.copy(gt_h[:], TB[:, 0:FC * P]).then_inc(s["gTh"], 1)

        def act_silu(sc, s, i):
            sc.wait_ge(s["G"], i + 1)
            if not known(i, 1):
                sc.wait_ge(s["g"], i)
            sc.activation(act[:], GB[:, 0:F], ACT.Silu).then_inc(s["act"], 1)

        def act_rows(sc, s, i):
            sc.wait_ge(s["rt"], i + 1)
            sc.copy(rt_h[:], XB[:, 0:D]).then_inc(s["rth"], 1)

        def dve_gt(v, s, i):
            v.wait_ge(s["gTh"], i + 1)
            v.tensor_tensor(gt_l[:], TB[:, 0:FC * P], gt_h[:].bitcast(F32), ALU.subtract).then_inc(s["gTl"], 1)

        def dve_g(v, s, i):
            v.wait_ge(s["act"], i + 1)
            v.wait_ge(s["U"], i + 1)
            if not known(i, 1):
                v.wait_ge(s["gT"], i)
            v.tensor_tensor(g[:, 0:F], UB[:, 0:F], act[:], ALU.mult).then_inc(s["g"], 1)

        def dve_rows(v, s, i):
            v.wait_ge(s["rth"], i + 1)
            v.tensor_tensor(rt_l[:], XB[:, 0:D], rt_h[:].bitcast(F32), ALU.subtract).then_inc(s["rtl"], 1)

        def pe_shared(pe, s, u, par, last=False, early=None, late=None):
            if not known(u, 1):
                pe_turn_g(pe, s, u * 2 - 1)
            pe_gate_up(pe, s, 0, u + 1)
            if not known(u, 1):
                pe_down(pe, s, u * 2 - 1, 1, False, True)
            if early:
                early()
            pe_turn_g(pe, s, u * 2)
            pe_gate_up(pe, s, 1, u + 1)
            if not last:
                pe_turn_rows(pe, s, u + 1, 1 - par)
            if late:
                late()
            if not known(u, 1):
                pe.wait_ge(s["y"], u)
            pe_down(pe, s, u * 2, 0, True, False)

        def pe_shared_end(pe, s, n):
            pe_turn_g(pe, s, 2 * n - 1)
            pe_down(pe, s, 2 * n - 1, 1, False, True)

        def act_shared(sc, s, u, last=False):
            if not known(u, 1):
                act_gt(sc, s, u * 2 - 1)
            act_silu(sc, s, u * 2)
            act_gt(sc, s, u * 2)
            act_silu(sc, s, u * 2 + 1)
            if not last:
                act_rows(sc, s, u + 1)

        @block.tensor
        def _(pe):
            pe.wait_ge(s_ident, 1)
            pe.wait_ge(s_cw, 16 * 10)
            for k in range(K):
                mm = pe.transpose(bank[3][:, k * E:(k + 1) * E], g_raw[:, k * P:(k + 1) * P], ident[0:E, 0:E])
            mm.then_inc(s_cwt, 1)
            for k in range(K):
                for o in range(K):
                    pe.transpose(bank[k][:, o * P:(o + 1) * P], base_raw[:, o, k * P:(k + 1) * P], ident[:])
                pe.transpose(bank[k][:, DX:DX + ER], a_raw[:, k * P:(k + 1) * P], ident[:])
                pe.transpose(bank[2][:, k * P:(k + 1) * P], b_raw[:, k, :], ident[:])
            pe.wait_ge(s_gate, 1)
            for k in range(K):
                for o in range(K):
                    pe.matmul(bank[k][:, D:DX], base_raw[:, o, k * P:(k + 1) * P], gate_t[:, o, :],
                              start=(o == 0), stop=(o == K - 1))
            for o in range(K):
                pe.matmul(bank[2][:, D:DX], b_raw[:, o, :], gate_t[:, o, :], start=(o == 0), stop=(o == K - 1))
            for o in range(K):
                mm = pe.matmul(bank[4][:, 0:E], b_col[:, o:o + 1].broadcast_to([P, P]), gate_t[:, o, :],
                               start=(o == 0), stop=(o == K - 1))
            mm.then_inc(s_cwf, 1)

            def turn_x(i, par):
                pe.wait_ge(s_xin[par // 2], quarter_of(i, par) * 16 + 16)
                for k in range(K):
                    mm = pe.transpose(TX[:, k * P:(k + 1) * P], xin[par // 2][:, par % 2, k * P:(k + 1) * P], ident[:])
                mm.then_inc(s_tx, 1)

            def main(i, par, k):
                if k == 0:
                    pe.wait_ge(s_txh, i + 1)
                    pe.wait_ge(s_txl, i + 1)
                    if not known(i, 4):
                        pe.wait_ge(s_lg, i - 3)
                mm = three_pass(pe, MAIN[par][:, 0:DX + ER], xt_h[par % 2][:, k * P:(k + 1) * P],
                                xt_l[par % 2][:, k * P:(k + 1) * P], wa_h[:, k, :], wa_l[:, k, :],
                                k == 0, k == K - 1)
                if k == K - 1:
                    mm.then_inc(s_main, 1)

            def turn_hw(i):
                pe.wait_ge(s_hw, i + 1)
                pe.transpose(THW[:, 0:P], hw[:], ident[:]).then_inc(s_thw, 1)

            def lora_out(i, par):
                pe.wait_ge(s_hwh, i + 1)
                pe.wait_ge(s_hwl, i + 1)
                three_pass(pe, MAIN[par][:, 0:DX], hw_h[:], hw_l[:], b_h[:], b_l[:], False, True,
                           skip=True).then_inc(s_p, 1)

            def step(i, par):
                main(i, par, 0)
                if not known(i, 1):
                    turn_hw(i - 1)
                if not (isinstance(i, int) and i + 1 >= NT):
                    turn_x(i + 1, (par + 1) % 4)
                main(i, par, 1)
                if not known(i, 1):
                    lora_out(i - 1, (par - 1) % 4)

            pe.wait_ge(s_cwh, 1)
            pe.wait_ge(s_cwl, 1)
            turn_x(0, 0)
            for i in range(4):
                step(i, i)
            turns(pe, 4, NT - 1, step, 4)
            step(NT - 1, (NT - 1) % 4)
            turn_hw(NT - 1)
            pe_turn_rows(pe, fp, 0, 0)
            lora_out(NT - 1, (NT - 1) % 4)

            def rank():
                pe.wait_ge(s_const, 1)
                pe.wait_ge(s_mark, 1)
                W = (NT + 1) * E
                pe.matmul(RANK_B[:, 0:W], tri[:], mark[:].rearrange("p t e -> p (t e)"), start=True, stop=True)
                for t in range(NT):
                    src = mark[:, t:t + 1, :].broadcast_to([P, NT - t, E])
                    mm = pe.matmul(RANK_B[:, (t + 1) * E:W], ones[:], src, start=False, stop=(t == NT - 1),
                                   skip_group_check=True)
                mm.then_inc(s_rank, 1)

            def perm(t, buf):
                pe.wait_ge(s_hot, t + 1)
                for c in range(TOPK):
                    mm = pe.matmul(PERM_B[:, 0:NBLKP], row_hot[c][buf][:], blk_hot[c][buf][:],
                                   start=isinstance(t, int) and t == 0 and c == 0,
                                   stop=isinstance(t, int) and t == NT - 1 and c == TOPK - 1)
                mm.then_inc(s_perm, 1)

            def perm_a(u):
                perm((u - HOT0) * 4, 0)
                perm((u - HOT0) * 4 + 1, 1)

            def perm_b(u):
                perm((u - HOT0) * 4 + 2, 2)
                perm((u - HOT0) * 4 + 3, 3)

            pe.wait_ge(s_wlo, 4 * NS)
            pe.wait_ge(s_lg, NT - 2)
            pe.wait_ge(s_gz, 1)
            for u in range(HOT0):
                pe_shared(pe, fp, u, u % 2, early=rank if u == RANK_AT else None)
            pe_shared(pe, fp, HOT0, HOT0 % 2, late=lambda: perm_a(HOT0))
            turns(pe, HOT0 + 1, HOT1, lambda u, par: pe_shared(
                pe, fp, u, par, early=lambda: perm_b(u - 1), late=lambda: perm_a(u)))
            for u in range(HOT1, NPRE):
                pe_shared(pe, fp, u, u % 2, last=(u == NPRE - 1), early=(lambda: perm_b(u - 1)) if u == HOT1 else None)
            pe_shared_end(pe, fp, NPRE)

            pe.wait_ge(s_routed, 1)
            pe.wait_ge(s_wlo, 4 * NE)

            def expert_of(i):
                return pe.value_load(blk_e[0:1, bass.ds(i, 1)], min_val=NS, max_val=NE - 1)

            def e_down(i, e):
                if not known(i, 1):
                    pe.wait_ge(fe["y"], i)
                pe_down(pe, fe, i, e, True, True)

            def e_step(i, par, e_prev, e):
                pe_turn_g(pe, fe, i - 1)
                pe_gate_up(pe, fe, e, i + 1)
                if not (isinstance(i, int) and i == NBLK - 1):
                    pe_turn_rows(pe, fe, i + 1, 1 - par)
                e_down(i - 1, e_prev)

            e0, e1 = expert_of(0), expert_of(1)
            pe.wait_ge(fp["y"], NPRE)
            pe_turn_rows(pe, fe, 0, 0)
            pe_gate_up(pe, fe, e0, 1)
            pe_turn_rows(pe, fe, 1, 1)
            e_step(1, 1, e0, e1)
            assert (NBLK - 3) % 4 == 0
            with pe.Fori(0, (NBLK - 3) // 4) as j:
                word = pe.value_load(blk_pack[0:1, bass.ds(j * 4 + 1, 1)], min_val=0, max_val=E ** 5 - 1)
                es = [((word >> (3 * d)) & (E - 1)) + NS for d in range(5)]
                for d in range(4):
                    e_step(j * 4 + (2 + d), d % 2, es[d], es[d + 1])
            ea, eb = expert_of(NBLK - 2), expert_of(NBLK - 1)
            e_step(NBLK - 1, (NBLK - 1) % 2, ea, eb)
            pe_turn_g(pe, fe, NBLK - 1)
            e_down(NBLK - 1, eb)

            n = NT - NPRE
            pe.wait_ge(fe["y"], NBLK)
            pe_turn_rows(pe, fs, 0, 0)
            pe_shared(pe, fs, 0, 0)
            turns(pe, 1, n - 1, lambda u, par: pe_shared(pe, fs, u, par))
            pe_shared(pe, fs, n - 1, (n - 1) % 2, last=True)
            pe_shared_end(pe, fs, n)

        @block.scalar
        def _(sc):
            def load_gu(n):
                shared = isinstance(n, int) and n < NS
                for w, sw, c in ((w_gate, sw_gate, 0), (w_up, sw_up, F)):
                    src = (sw[:, n * F:(n + 1) * F].rearrange("(k p) f -> p k f", p=P) if shared else
                           w[bass.ds(n - NS, 1)].rearrange("e (k p) f -> p (e k) f", p=P))
                    sc.dma_start(gu_own[:, bass.ds(n, 1), :, c:c + F].rearrange("p e k f -> p (e k) f"),
                                 src).then_inc(s_raw[0], 16)

            def load_dn(n):
                shared = isinstance(n, int) and n < NS
                src = (sw_down[n * F:(n + 1) * F, :] if shared else
                       w_down[bass.ds(n - NS, 1)].rearrange("e f d -> (e f) d"))
                sc.dma_start(dn_own[:, bass.ds(n, 1), 0:FULL, :].rearrange("p e c d -> p (e c) d"),
                             src[0:FULL * P, :].rearrange("(c p) d -> p c d", p=P)).then_inc(s_raw[1], 16)
                sc.dma_start(dn_own[0:REST, bass.ds(n, 1), FULL, :].rearrange("p e d -> p (e d)"),
                             src[FULL * P:F, :]).then_inc(s_raw[1], 16)

            load_gu(0)
            load_dn(0)
            sc.wait_ge(s_ident, 1)
            sc.activation(spare[0:1, 2:3], ident[0:1, 0:1], ACT.Silu)
            sc.wait_ge(s_cwt, 1)
            sc.copy(gate_t[:].rearrange("p k e -> p (k e)"), bank[3][:, 0:K * E]).then_inc(s_gate, 1)
            sc.wait_ge(s_cwf, 1)
            for k in range(K):
                sc.copy(wa_h[:, k, :], bank[k][:, 0:DX + ER])
            sc.copy(bias[:, D:DX], bank[4][:, 0:E])
            sc.copy(b_h[:], bank[2][:, 0:DX]).then_inc(s_cwh, 1)

            def a_x(i, par):
                sc.wait_ge(s_tx, i + 1)
                if not known(i, 2):
                    sc.wait_ge(s_main, i - 1)
                sc.copy(xt_h[par % 2][:], TX[:, 0:D]).then_inc(s_txh, 1)

            def a_hw(i):
                sc.wait_ge(s_thw, i + 1)
                sc.copy(hw_h[:], THW[:, 0:P]).then_inc(s_hwh, 1)

            def high_parts(n, u, last=False):
                if u == 0:
                    sc.wait_ge(s_raw[0], n * 32 + 32)
                if u == K:
                    sc.wait_ge(s_raw[1], n * 32 + 32)
                for p, (own_ap, hi, _) in enumerate(weight_parts(n)):
                    if p == u or (u == K and p > K):
                        sc.copy(hi, own_ap).then_inc(s_whi, 1)
                if not last and u == K - 1:
                    load_gu(n + 1)
                if not last and u == K:
                    load_dn(n + 1)

            def step(i, par):
                if not known(i, 1):
                    a_hw(i - 1)
                if not (isinstance(i, int) and i + 1 >= NT):
                    a_x(i + 1, par + 1)
            a_x(0, 0)
            for n in range(NS):
                for u in range(4):
                    step(4 * n + u, u)
                    if u <= K:
                        high_parts(n, u)
            with sc.Fori(NS, NT // 4 - 1) as n:
                for u in range(4):
                    step(n * 4 + u, u)
                    if u <= K:
                        high_parts(n, u)
            n_proj = NT // 4
            for u in range(4):
                step(NT - 4 + u, u)
                if u <= K:
                    high_parts(n_proj - 1, u)
            a_hw(NT - 1)
            act_rows(sc, fp, 0)

            def high_all(n):
                for u in range(K + 1):
                    high_parts(n, u, last=(n == NE - 1))
            act_shared(sc, fp, 0)
            high_all(n_proj)
            sc.wait_ge(s_exp_in, 1)
            sc.activation(prob[:], pos[:], ACT.Exp).then_inc(s_exp, 1)
            for u in range(1, NE - n_proj):
                act_shared(sc, fp, u)
                high_all(n_proj + u)
            turns(sc, NE - n_proj, NPRE - 1, lambda u, par: act_shared(sc, fp, u))
            act_shared(sc, fp, NPRE - 1, last=True)
            act_gt(sc, fp, 2 * NPRE - 1)

            for p in range(2):
                sc.wait_ge(s_bout[p], 16 * (NPRE // 2))

            def e_y(i, par):
                sc.wait_ge(fe["D"], i + 1)
                if not known(i, 2):
                    sc.wait_ge(s_yst[par], half_of(i, par) * 16)
                sc.copy(y_sb[par][:], YB[:, 0:D]).then_inc(fe["y"], 1)

            def e_step(i, par):
                act_gt(sc, fe, i - 1)
                act_silu(sc, fe, i)
                if not (isinstance(i, int) and i == NBLK - 1):
                    act_rows(sc, fe, i + 1)
                e_y(i - 1, 1 - par)
            act_rows(sc, fe, 0)
            act_silu(sc, fe, 0)
            act_rows(sc, fe, 1)
            for i in (1, 2):
                e_step(i, i % 2)
            turns(sc, 3, NBLK - 1, e_step)
            e_step(NBLK - 1, (NBLK - 1) % 2)
            act_gt(sc, fe, NBLK - 1)
            e_y(NBLK - 1, (NBLK - 1) % 2)

            n = NT - NPRE
            act_rows(sc, fs, 0)
            act_shared(sc, fs, 0)
            turns(sc, 1, n - 1, lambda u, par: act_shared(sc, fs, u))
            act_shared(sc, fs, n - 1, last=True)
            act_gt(sc, fs, 2 * n - 1)

        @block.vector
        def _(v):
            v.wait_ge(s_cwh, 1)
            for k in range(K):
                v.tensor_tensor(wa_l[:, k, :], bank[k][:, 0:DX + ER], wa_h[:, k, :].bitcast(F32), ALU.subtract)
            v.tensor_tensor(b_l[:], bank[2][:, 0:DX], b_h[:].bitcast(F32), ALU.subtract).then_inc(s_cwl, 1)

            def v_x(i, par):
                v.wait_ge(s_txh, i + 1)
                v.tensor_tensor(xt_l[par % 2][:], TX[:, 0:D], xt_h[par % 2][:].bitcast(F32),
                                ALU.subtract).then_inc(s_txl, 1)

            def v_hw(i, par):
                v.wait_ge(s_main, i + 1)
                w = w_tok[:, bass.ds(i, 1), :].rearrange("p t (e r) -> p (t e) r", r=1).broadcast_to([P, E, RANK])
                v.scalar_tensor_tensor(out=hw[:].rearrange("p (e r) -> p e r", e=E),
                                       in0=MAIN[par][:, DX:DX + ER].rearrange("p (e r) -> p e r", e=E),
                                       scalar=LORA_SCALING, in1=w, op0=ALU.mult, op1=ALU.mult).then_inc(s_hw, 1)

            def v_hwl(i):
                v.wait_ge(s_hwh, i + 1)
                v.tensor_tensor(hw_l[:], THW[:, 0:P], hw_h[:].bitcast(F32), ALU.subtract).then_inc(s_hwl, 1)

            def v_x1(i, par):
                v.wait_ge(s_p, i + 1)
                if not known(i, 4) and par % 2 == 0:
                    v.wait_ge(s_x1st[par // 2], quarter_of(i, par) * 16)
                v.tensor_tensor(x1[par // 2][:, par % 2, :], MAIN[par][:, 0:D], bias[:, 0:D], ALU.add).then_inc(s_x1, 1)
                v.tensor_tensor(logits[:, bass.ds(i, 1), :].rearrange("p t e -> p (t e)"), MAIN[par][:, D:DX],
                                bias[:, D:DX], ALU.add).then_inc(s_lg, 1)

            def step(i, par):
                if not known(i, 1):
                    v_hwl(i - 1)
                if not (isinstance(i, int) and i + 1 >= NT):
                    v_x(i + 1, par + 1)
                v_hw(i, par)
                if not known(i, 1):
                    v_x1(i - 1, (par - 1) % 4)
            v_x(0, 0)
            for i in range(4):
                step(i, i)
            turns(v, 4, NT - 1, step, 4)
            step(NT - 1, (NT - 1) % 4)
            v_hwl(NT - 1)
            dve_rows(v, fp, 0)
            v_x1(NT - 1, (NT - 1) % 4)

            count = [0]

            def link(ins):
                count[0] += 1
                ins.then_inc(s_r, 1)
                v.wait_ge(s_r, count[0])

            def over_e(a):
                return a[:].rearrange("p (t o) -> p t o", o=1).broadcast_to([P, NT, E])

            def routing():
                v.wait_ge(s_const, 1)
                for p in range(2):
                    v.wait_ge(s_x1st[p], 16 * (NT // 4))
                v.wait_ge(s_lg, NT)
                yield link(v.tensor_reduce(red[:], logits[:], AX.X, ALU.max))
                yield v.tensor_tensor(pos[:], logits[:], over_e(red), ALU.subtract).then_inc(s_exp_in, 1)
                yield "exp"
                v.wait_ge(s_exp, 1)
                yield link(v.tensor_reduce(red[:], prob[:], AX.X, ALU.add))
                yield link(v.reciprocal(red[:], red[:]))
                yield link(v.tensor_tensor(prob[:], prob[:], over_e(red), ALU.mult))
                for c, p in enumerate((prob, prob2)):
                    yield link(v.tensor_reduce(top_v[c][:], p[:], AX.X, ALU.max))
                    yield link(v.tensor_tensor(tmp[:], p[:], over_e(top_v[c]), ALU.is_equal))
                    yield link(v.tensor_tensor(tmp[:], tmp[:], down_e[:].rearrange("p (o e) -> p o e", o=1)
                                               .broadcast_to([P, NT, E]), ALU.mult))
                    yield link(v.tensor_reduce(red[:], tmp[:], AX.X, ALU.max))
                    yield link(v.tensor_tensor(hot[c][:], tmp[:], over_e(red), ALU.is_equal))
                    if c == 0:
                        yield link(v.scalar_tensor_tensor(out=prob2[:].rearrange("p t e -> p (t e)"),
                                                          in0=hot[0][:].rearrange("p t e -> p (t e)"), scalar=-2.0,
                                                          in1=prob[:].rearrange("p t e -> p (t e)"),
                                                          op0=ALU.mult, op1=ALU.add))
                yield v.tensor_tensor(mark[:, 0:NT, :], hot[0][:], hot[1][:], ALU.add).then_inc(s_mark, 1)
                yield link(v.tensor_tensor(red[:], top_v[0][:], top_v[1][:], ALU.add))
                yield link(v.tensor_scalar(red[:], red[:], 1e-20, None, ALU.add))
                yield link(v.reciprocal(red[:], red[:]))
                for c in range(TOPK):
                    yield link(v.tensor_tensor(top_w[c][:], top_v[c][:], red[:], ALU.mult))
                    yield link(v.tensor_scalar(top_w[c][:], top_w[c][:], ROUTED_SCALE, None, ALU.mult))
                v.wait_ge(s_rank, 1)
                yield link(v.tensor_copy(nb[:], RANK_B[:, NT * E:(NT + 1) * E]))
                yield link(v.tensor_tensor(over[:], nb[:].rearrange("p (e o) -> p e o", o=1).broadcast_to([P, E, NT]),
                                           step128[:].rearrange("p (o t) -> p o t", o=1).broadcast_to([P, E, NT]),
                                           ALU.is_gt))
                yield link(v.tensor_reduce(nb[:], over[:], AX.X, ALU.add))
                yield link(v.tensor_tensor(ee[:], upto[:],
                                           nb[:].rearrange("p (o e) -> p o e", o=1).broadcast_to([P, E, E]), ALU.mult))
                yield link(v.tensor_reduce(bend[:], ee[:], AX.X, ALU.add))
                yield link(v.tensor_tensor(bbase[:], bend[:], nb[:], ALU.subtract))
                yield link(v.tensor_scalar(bbase[:], bbase[:], float(P), None, ALU.mult))
                yield link(v.tensor_tensor(pos[:], RANK_B[:, 0:NT * E].rearrange("p (t e) -> p t e", e=E),
                                           bbase[:].rearrange("p (o e) -> p o e", o=1).broadcast_to([P, NT, E]),
                                           ALU.add))
                for c in range(TOPK):
                    yield link(v.tensor_tensor(prob[:], pos[:], hot[c][:], ALU.mult))
                    yield link(v.tensor_reduce(slot_f[:, c, :], prob[:], AX.X, ALU.add))
                yield link(v.tensor_copy(slot_i[:], slot_f[:]))
                yield link(v.tensor_scalar(part_i[:], slot_i[:], 7, None, ALU.logical_shift_right))
                yield link(v.tensor_copy(blk_of[:], part_i[:]))
                yield link(v.tensor_scalar(part_i[:], slot_i[:], P - 1, None, ALU.bitwise_and))
                yield link(v.tensor_copy(row_of[:], part_i[:]))
                yield link(v.tensor_tensor(blk_cmp[:],
                                           iota_blk[0:1, :].rearrange("p (b o) -> p b o", o=1)
                                           .broadcast_to([1, NBLKP, E]),
                                           bend[0:1, :].rearrange("p (o e) -> p o e", o=1).broadcast_to([1, NBLKP, E]),
                                           ALU.is_ge))
                yield link(v.tensor_reduce(blk_ef[:], blk_cmp[:], AX.X, ALU.add))
                yield link(v.tensor_scalar(blk_ef[:], blk_ef[:], float(E - 1), None, ALU.min))
                yield link(v.tensor_scalar(blk_e[:], blk_ef[:], float(NS), None, ALU.add))
                W = NBLKP - 4
                yield link(v.tensor_copy(pack_f[:, 0:W], blk_ef[:, 4:NBLKP]))
                for d in (3, 2, 1, 0):
                    yield link(v.scalar_tensor_tensor(out=pack_f[:, 0:W], in0=pack_f[:, 0:W], scalar=float(E),
                                                      in1=blk_ef[:, d:d + W], op0=ALU.mult, op1=ALU.add))
                yield link(v.tensor_copy(blk_pack[:, 0:W], pack_f[:, 0:W]))

            def wait_x(u, par):
                v.wait_ge(s_bres[par], half_of(u, par) * 16 + 16)

            todo = routing()

            def some(n):
                for _ in range(n):
                    if next(todo, None) == "exp":
                        break

            def final(s, u, par, counted):
                v.wait_ge(s["D"], u * 2 + 2)
                if not known(u, 2):
                    v.wait_ge(counted[par], half_of(u, par) * 16)
                v.tensor_tensor(y_sb[par][:], YB[:, 0:D], res[par][:], ALU.add).then_inc(s["y"], 1)

            def shared(s, u, par, counted, last=False, mid=None, end=None):
                if not known(u, 1):
                    dve_gt(v, s, u * 2 - 1)
                dve_g(v, s, u * 2)
                if not known(u, 1):
                    final(s, u - 1, 1 - par, counted)
                if mid:
                    mid()
                dve_gt(v, s, u * 2)
                dve_g(v, s, u * 2 + 1)
                if not last:
                    dve_rows(v, s, u + 1)
                if end:
                    end()

            def base_tile(u, par, last=False, mid=None, end=None):
                shared(fp, u, par, s_bout, last, mid, end)

            def hot_pair(u, k):
                for q in range(2):
                    hots(v, (u - HOT0) * 4 + (2 * k + q), 2 * k + q)

            for u in range(HOT0):
                if u:
                    wait_x(u - 1, 1 - u % 2)
                base_tile(u, u % 2, mid=lambda: some(MATH), end=lambda: some(MATH))
            some(100)

            def hot_tile(u, par):
                wait_x(u - 1, 1 - par)
                base_tile(u, par, mid=lambda: hot_pair(u, 0), end=lambda: hot_pair(u, 1))
            hot_tile(HOT0, HOT0 % 2)
            turns(v, HOT0 + 1, HOT1, hot_tile)

            def list_out():
                v.wait_ge(s_perm, NT)
                v.tensor_copy(perm_i[:], PERM_B[:, 0:NBLKP]).then_inc(s_routed, 1)
            for u in range(HOT1, NPRE):
                wait_x(u - 1, 1 - u % 2)
                base_tile(u, u % 2, last=(u == NPRE - 1), mid=list_out if u == HOT1 else None)
            dve_gt(v, fp, 2 * NPRE - 1)
            wait_x(NPRE - 1, (NPRE - 1) % 2)
            final(fp, NPRE - 1, (NPRE - 1) % 2, s_bout)

            def e_step(i, par):
                dve_gt(v, fe, i - 1)
                dve_g(v, fe, i)
                if not (isinstance(i, int) and i == NBLK - 1):
                    dve_rows(v, fe, i + 1)
            dve_rows(v, fe, 0)
            dve_g(v, fe, 0)
            dve_rows(v, fe, 1)
            e_step(1, 1)
            turns(v, 2, NBLK - 1, e_step)
            e_step(NBLK - 1, (NBLK - 1) % 2)
            dve_gt(v, fe, NBLK - 1)

            def add_picks(to, picks, t, counted, n):
                for c in range(TOPK):
                    v.scalar_tensor_tensor(out=to[:], in0=picks[c][:], scalar=top_w[c][:, bass.ds(t, 1)],
                                           in1=to[:], op0=ALU.mult, op1=ALU.add).then_inc(counted, 1)
                    if c == 0:
                        v.wait_ge(counted, n + 1)

            def mix(u, par, to):
                v.wait_ge(s_pick[par], half_of(u, par) * 32 + 32)
                add_picks(to, [pick[c][par] for c in range(TOPK)], u + NPRE, s_mix, u * 2)

            def mix_early(q, par):
                v.wait_ge(s_eres[par], half_of(q, par) * 16 + 16)
                v.wait_ge(s_epick[par], half_of(q, par) * 32 + 32)
                add_picks(e_res[par], [e_pick[c][par] for c in range(TOPK)], q, s_emix, q * 2)

            def out_tile(m, par, q, q_par):
                def end():
                    v.wait_ge(fs["y"], m + 1)
                    mix(m, par, y_sb[par])
                    if q is not None:
                        mix_early(q, q_par)
                v.wait_ge(s_res[par], half_of(m, par) * 16 + 16)
                shared(fs, m + 1, 1 - par, s_out, end=end)
            dve_rows(v, fs, 0)
            shared(fs, 0, 0, s_out)
            v.wait_ge(s_yst[0], 16 * ((NBLK + 1) // 2))
            v.wait_ge(s_yst[1], 16 * (NBLK // 2))
            with_early(v, out_tile)
            n = NT - NPRE

            def end():
                v.wait_ge(fs["y"], n - 1)
                mix(n - 2, n % 2, y_sb[n % 2])
                v.wait_ge(s_res[(n - 1) % 2], (n - 1) // 2 * 16 + 16)
                mix(n - 1, (n - 1) % 2, res[(n - 1) % 2])
            v.wait_ge(s_res[n % 2], (n - 2) // 2 * 16 + 16)
            shared(fs, n - 1, (n - 1) % 2, s_out, last=True, end=end)
            dve_gt(v, fs, 2 * n - 1)
            v.wait_ge(s_mix, 2 * n)
            final(fs, n - 1, (n - 1) % 2, s_out)


_INS = ['x', 'cond_8', 'L0_cond_W_base', 'L0_cond_b_base', 'L0_cond_As', 'L0_cond_Bs', 'L0_ffn_gate_w',
        'L0_ffn_w_gate', 'L0_ffn_w_up', 'L0_ffn_w_down', 'L0_ffn_sw_gate', 'L0_ffn_sw_up', 'L0_ffn_sw_down']


def kernel(**inputs):
    import numpy as _np
    import concourse.bacc as _bacc
    from concourse import mybir as _mybir
    from concourse.bass_utils import run_bass_kernel_spmd as _run

    nc = _bacc.Bacc("TRN2", target_bir_lowering=False, num_devices=1)
    arrays, args = {}, []
    for name in _INS:
        a = _np.ascontiguousarray(inputs[name])
        arrays[f"in_{name}_dram"] = a
        args.append(nc.dram_tensor(f"in_{name}_dram", a.shape, _mybir.dt.from_np(a.dtype), kind="ExternalInput").ap())
    args.append(nc.dram_tensor("out_0_dram", inputs['x'].shape, _mybir.dt.float32, kind="ExternalOutput").ap())
    adaln_moe(nc, *args)
    r = _run(nc, [arrays], core_ids=[0])
    return r.results[0]["out_0_dram"]
```

```python
from contextlib import ExitStack

import concourse.bass as bass
from concourse import mybir

F32 = mybir.dt.float32
F32R = mybir.dt.float32r
BF16 = mybir.dt.bfloat16
I32 = mybir.dt.int32
U32 = mybir.dt.uint32
ALU = mybir.AluOpType
ACT = mybir.ActivationFunctionType
AX = mybir.AxisListType

P = 128
TOPK = 2
LORA_SCALING = 2.0
ROUTED_SCALE = 2.5


def adaln_moe(nc, x, cond, w_base, b_base, lora_a, lora_b, gate_w, w_gate, w_up, w_down,
              sw_gate, sw_up, sw_down, out):
    NB, SEQ, D = x.shape
    E, RANK, _ = lora_a.shape
    F = w_gate.shape[2]
    T = NB * SEQ
    NT = T // P
    K = D // P
    ER = E * RANK
    NS = sw_gate.shape[1] // F
    NE = E + NS
    FULL = F // P
    REST = F - FULL * P
    FC = FULL + 1
    NBLK = (TOPK * T + E * (P - 1)) // P
    NBLKP = NBLK + NBLK % 2
    DX = D + E
    HOT0 = 5
    HOT1 = HOT0 + NT // 4
    NPRE = HOT1 + 1
    FIN_A = 3 * NPRE - NT + 2
    TURN = 6
    RANK_AT = 4
    MATH = ((0, 0, 0, 4), (0, 0, 4, 3), (4, 3, 4, 3), (4, 3, 4, 1), (0, 7, 6, 6))
    assert len(MATH) == HOT0 and NPRE % 2 == 0 and FIN_A % 2 == 0 and FIN_A >= 2 and NPRE > FIN_A
    assert SEQ * 2 == P and K == 2 and ER == P and NS == 2 and E == 8 and REST > 0

    x_rows = x.rearrange("b s d -> (b s) d")
    out_rows = out.rearrange("b s d -> (b s) d")
    x1_dram = nc.dram_tensor("x1_rows", (T, D), F32, kind="Internal").ap()
    y_dram = nc.dram_tensor("y_slots", (NBLK * P, D), F32, kind="Internal").ap()

    base_dram = nc.dram_tensor("base_rows", (NPRE * P, D), F32, kind="Internal").ap()

    with ExitStack() as ctx:
        def sb(name, shape, dt=F32, where=ctx):
            return where.enter_context(nc.sbuf_tensor(name, shape, dt))

        def sem(name):
            return ctx.enter_context(nc.semaphore(name))

        bank = [ctx.enter_context(nc.psum_tensor(f"bank{i}", [P, 512], F32)) for i in range(8)]

        gu_h = sb("gu_h", [P, NE, K, 2 * F], F32R)
        dn_h = sb("dn_h", [P, NE, FC, D], F32R)
        with ExitStack() as own:
            gu_own = sb("gu_own", [P, NE, K, 2 * F], F32, own)
            dn_own = sb("dn_own", [P, NE, FC, D], F32, own)
        gu_l = sb("gu_l", [P, NE, K, 2 * F], F32R)
        dn_l = sb("dn_l", [P, NE, FC, D], F32R)
        ident = sb("ident", [P, P])
        spare = sb("spare", [1, 4])
        logits = sb("logits", [P, NT, E])
        top_w = [sb(f"top_w{c}", [P, NT]) for c in range(TOPK)]
        slot_i = sb("slot_i", [P, TOPK, NT], I32)
        perm_i = sb("perm_i", [P, NBLKP], I32)
        blk_e = sb("blk_e", [1, NBLKP], I32)
        rows = [sb(f"rows{i}", [P, D]) for i in range(2)]
        rt_h = sb("rt_h", [P, D], F32R)
        rt_l = sb("rt_l", [P, D], F32R)
        act = sb("act", [P, F])
        g = sb("g", [P, FC * P])
        down_e = sb("down_e", [P, E])
        tri = sb("tri", [P, P], BF16)
        ones = sb("ones", [P, P], BF16)
        step128 = sb("step128", [P, NT])
        upto = sb("upto", [P, E, E])
        iota_row = sb("iota_row", [P, P])
        iota_blk = sb("iota_blk", [P, NBLKP])
        tok_id = sb("tok_id", [P, NT])
        PAD = NT // 2
        mark = sb("mark", [P, PAD + NT + 1, E], BF16)

        with ExitStack() as proj:
            wa_h = sb("wa_h", [P, K, DX + ER], F32R, proj)
            wa_l = sb("wa_l", [P, K, DX + ER], F32R, proj)
            b_h = sb("b_h", [P, DX], F32R, proj)
            b_l = sb("b_l", [P, DX], F32R, proj)
            bias = sb("bias", [P, DX], F32, proj)
            w_tok = sb("w_tok", [P, NT, E], F32, proj)
            xin = [sb(f"xin{i}", [P, D], F32, proj) for i in range(4)]
            hw = sb("hw", [P, ER], F32, proj)
            hw_h = sb("hw_h", [P, P], F32R, proj)
            hw_l = sb("hw_l", [P, P], F32R, proj)
            with ExitStack() as raw:
                base_raw = sb("base_raw", [P, K, D], F32, raw)
                a_raw = sb("a_raw", [P, D], F32, raw)
                b_raw = sb("b_raw", [P, K, ER], F32, raw)
                g_raw = sb("g_raw", [E, D], F32, raw)
                gate_t = sb("gate_t", [P, K, E], F32, raw)
                b_col = sb("b_col", [P, K], F32, raw)
            xt_h = [sb(f"xt_h{i}", [P, D], F32R, proj) for i in range(2)]
            xt_l = [sb(f"xt_l{i}", [P, D], F32R, proj) for i in range(2)]
            x1 = [sb(f"x1_{i}", [P, 2, D], F32, proj) for i in range(2)]
        with ExitStack() as ffn:
            gt_h = sb("gt_h", [P, FC * P], F32R, ffn)
            gt_l = sb("gt_l", [P, FC * P], F32R, ffn)
            y_sb = [sb(f"y_sb{i}", [P, D], F32, ffn) for i in range(2)]
            res = [sb(f"res{i}", [P, D], F32, ffn) for i in range(2)]
            with ExitStack() as route:
                R3 = [P, NT, E]
                with ExitStack() as math:
                    prob = sb("prob", R3, F32, math)
                    prob2 = sb("prob2", R3, F32, math)
                    pos = sb("pos", R3, F32, math)
                    tmp = sb("tmp", R3, BF16, math)
                    hot = [sb(f"hot{c}", R3, BF16, math) for c in range(TOPK)]
                    upto_tile = [sb(f"upto_tile{i}", [P, PAD + NT, E], BF16, math) for i in range(2)]
                row_hot = [[sb(f"row_hot{c}_{i}", [P, P], F32R, route) for i in range(4)] for c in range(TOPK)]
                blk_hot = [[sb(f"blk_hot{c}_{i}", [P, NBLKP], F32R, route) for i in range(4)] for c in range(TOPK)]
                red = sb("red", [P, NT], F32, route)
                top_v = [sb(f"top_v{c}", [P, NT], F32, route) for c in range(TOPK)]
                ee = sb("ee", [P, E, E], F32, route)
                nb = sb("nb", [P, E], F32, route)
                bend = sb("bend", [P, E], F32, route)
                bbase = sb("bbase", [P, E], F32, route)
                slot_f = sb("slot_f", [P, TOPK, NT], F32, route)
                part_i = sb("part_i", [P, TOPK, NT], I32, route)
                blk_of = sb("blk_of", [P, TOPK, NT], F32, route)
                row_of = sb("row_of", [P, TOPK, NT], F32, route)
                blk_cmp = sb("blk_cmp", [1, NBLKP, E], BF16, route)
                blk_ef = sb("blk_ef", [1, NBLKP], F32, route)
            idx = [sb(f"idx{i}", [P, 1], I32, ffn) for i in range(2)]
            pick = [[sb(f"pick{c}_{i}", [P, D], F32, ffn) for i in range(2)] for c in range(TOPK)]
            pidx = [[sb(f"pidx{c}_{i}", [P, 1], I32, ffn) for i in range(2)] for c in range(TOPK)]
            e_res = [sb(f"e_res{i}", [P, D], F32, ffn) for i in range(2)]
            e_pick = [[sb(f"e_pick{c}_{i}", [P, D], F32, ffn) for i in range(2)] for c in range(TOPK)]
            e_pidx = [[sb(f"e_pidx{c}_{i}", [P, 1], I32, ffn) for i in range(2)] for c in range(TOPK)]

        s_ident = sem("s_ident")
        s_const = sem("s_const")
        s_cw, s_cb = sem("s_cw"), sem("s_cb")
        s_cx = sem("s_cx")
        s_cwt, s_gate, s_cwf = sem("s_cwt"), sem("s_gate"), sem("s_cwf")
        s_cwh, s_cwl = sem("s_cwh"), sem("s_cwl")
        s_raw = [sem(f"s_raw{u}") for u in range(2)]
        s_raw_end = [sem(f"s_raw_end{u}") for u in range(2)]
        s_whi, s_wlo = sem("s_whi"), sem("s_wlo")
        s_pool = sem("s_pool")

        s_xin = [sem(f"s_xin{i}") for i in range(4)]
        s_tx, s_txh, s_txl = sem("s_tx"), sem("s_txh"), sem("s_txl")
        s_main, s_hw, s_thw = sem("s_main"), sem("s_hw"), sem("s_thw")
        s_hwh, s_hwl = sem("s_hwh"), sem("s_hwl")
        s_p, s_x1, s_lg = sem("s_p"), sem("s_x1"), sem("s_lg")
        s_x1st = [sem(f"s_x1st{i}") for i in range(2)]

        s_r, s_exp, s_exp_in, s_gz = sem("s_r"), sem("s_exp"), sem("s_exp_in"), sem("s_gz")
        s_mark, s_sums, s_rank = sem("s_mark"), sem("s_sums"), sem("s_rank")
        s_hot = sem("s_hot")
        s_perm, s_routed, s_blk = sem("s_perm"), sem("s_routed"), sem("s_blk")

        def ffn_sems(tag):
            names = "row rt rth rtl G U act g gT gTh gTl D y".split()
            return {n: [sem(f"{tag}_{n}{i}") for i in range(2)] if n == "row" else sem(f"{tag}_{n}")
                    for n in names}

        fp, fe, fs = ffn_sems("pre"), ffn_sems("ex"), ffn_sems("post")
        s_yst = [sem(f"s_yst{i}") for i in range(2)]
        s_idx = sem("s_idx")
        s_bres = [sem(f"s_bres{i}") for i in range(2)]
        s_bout = [sem(f"s_bout{i}") for i in range(2)]
        s_res = [sem(f"s_res{i}") for i in range(2)]
        s_pick = [sem(f"s_pick{i}") for i in range(2)]
        s_pidx, s_mix = sem("s_pidx"), sem("s_mix")
        s_out = [sem(f"s_out{i}") for i in range(2)]
        s_epidx, s_emix = sem("s_epidx"), sem("s_emix")
        s_eres, s_epick, s_eout = ([sem(f"s_e{n}{i}") for i in range(2)] for n in "res pick out".split())

        block = ctx.enter_context(nc.Block())

        TX, MAIN, THW = bank[0], bank[1:5], bank[5]
        XB, GB, UB, TB, YB, RANK_B, PERM_B = bank[0], bank[1], bank[2], bank[3], bank[4], bank[6], bank[7]

        def known(i, below):
            return isinstance(i, int) and i < below

        def three_pass(pe, o, lh, ll, rh, rl, start, stop, skip=False):
            pe.matmul(o, lh, rh, start=start, stop=False, skip_group_check=skip)
            pe.matmul(o, lh, rl, start=False, stop=False, skip_group_check=skip)
            return pe.matmul(o, ll, rh, start=False, stop=stop, skip_group_check=skip)

        def turns(eng, lo, hi, step, n=2, after=None):
            count = (hi - lo) // n
            if count:
                with eng.Fori(0, count) as j:
                    for u in range(n):
                        step(j * n + (lo + u), (lo + u) % n)
                        if after:
                            after(j, u)
            for i in range(lo + n * count, hi):
                step(i, i % n)

        def with_early(eng, step):
            def one(m, par):
                step(m, par, (m, par), None if known(m, 1) else (m - 1, 1 - par))
            one(0, 0)
            one(1, 1)
            turns(eng, 2, FIN_A, one)
            last_q = (FIN_A - 1, 1)
            for m in range(FIN_A, NT - NPRE - 2):
                q = (FIN_A + (m - FIN_A) // 2, (m - FIN_A) // 2 % 2) if m % 2 == 0 else None
                step(m, m % 2, q, last_q)
                last_q = q

        def half_of(i, par):
            return i // 2 if isinstance(i, int) else (i - par % 2) // 2

        def quarter_of(i, par):
            return i // 4 if isinstance(i, int) else (i - par) // 4

        def weight_parts(e):
            for k in range(K):
                yield tuple(w[:, bass.ds(e, 1), k, :].rearrange("p e f -> p (e f)") for w in (gu_own, gu_h, gu_l))
            yield tuple(w[:, bass.ds(e, 1), 0:FULL, :].rearrange("p e c d -> p (e c d)") for w in (dn_own, dn_h, dn_l))
            yield tuple(w[0:REST, bass.ds(e, 1), FULL, :].rearrange("p e d -> p (e d)") for w in (dn_own, dn_h, dn_l))

        def hots(v, t, buf):
            if not known(t, 4):
                v.wait_ge(s_perm, t - 3)
            for c in range(TOPK):
                v.tensor_scalar(row_hot[c][buf][:], iota_row[:], row_of[:, c, bass.ds(t, 1)], None, ALU.is_equal)
                ins = v.tensor_scalar(blk_hot[c][buf][:], iota_blk[:], blk_of[:, c, bass.ds(t, 1)],
                                      tok_id[:, bass.ds(t, 1)], ALU.is_equal, ALU.mult)
            ins.then_inc(s_hot, 1)

        @block.sync
        def _(sp):
            sp.dma_start(g_raw[:], gate_w).then_inc(s_cw, 16)
            sp.dma_start(base_raw[:], w_base.rearrange("(k p) c -> p k c", p=P)).then_inc(s_cw, 16)
            sp.dma_start(a_raw[:], lora_a.rearrange("e r c -> (e r) c")).then_inc(s_cw, 16)
            for k in range(K):
                sp.dma_start(b_raw[:, k, :].rearrange("p (e r) -> p e r", e=E),
                             lora_b[:, k * P:(k + 1) * P, :].rearrange("e o r -> o e r")).then_inc(s_cb, 16)
            for k in range(K):
                sp.dma_start(b_col[:, k:k + 1], b_base[k * P:(k + 1) * P].rearrange("(p a) -> p a", a=1)
                             ).then_inc(s_cb, 16)

            def load_rows(s, t, par, first):
                if not known(t, first + 2):
                    sp.wait_ge(s["rt"], t - (first + 1))
                sp.dma_start(rows[par][:], x1_dram[bass.ds(t * P, P), :]).then_inc(s["row"][par], 16)

            def load_x(t, par):
                if not known(t, 4):
                    sp.wait_ge(s_tx, t - 3)
                sp.dma_start(xin[par][:], x_rows[bass.ds(t * P, P), :]).then_inc(s_xin[par], 16)

            def store_x1(t, buf):
                sp.wait_ge(s_x1, t + 2)
                sp.dma_start(x1_dram[bass.ds(t * P, 2 * P), :].rearrange("(t p) d -> p t d", p=P),
                             x1[buf][:]).then_inc(s_x1st[buf], 16)

            def landed(n, u):
                if known(n, NE) and n == NE - 1:
                    return s_raw_end[u]
                if not known(n, 1):
                    sp.wait_ge(s_whi, n * 4 - (3 if u == 0 else 1))
                return s_raw[u]

            def load_gu(n):
                done = landed(n, 0)
                for w, sw, c in ((w_gate, sw_gate, 0), (w_up, sw_up, F)):
                    src = (sw[:, n * F:(n + 1) * F].rearrange("(k p) f -> p k f", p=P) if known(n, NS) else
                           w[bass.ds(n - NS, 1)].rearrange("e (k p) f -> p (e k) f", p=P))
                    sp.dma_start(gu_own[:, bass.ds(n, 1), :, c:c + F].rearrange("p e k f -> p (e k) f"),
                                 src).then_inc(done, 16)

            def load_dn(n):
                done = landed(n, 1)
                src = (sw_down[n * F:(n + 1) * F, :] if known(n, NS) else
                       w_down[bass.ds(n - NS, 1)].rearrange("e f d -> (e f) d"))
                sp.dma_start(dn_own[:, bass.ds(n, 1), 0:FULL, :].rearrange("p e c d -> p (e c) d"),
                             src[0:FULL * P, :].rearrange("(c p) d -> p c d", p=P)).then_inc(done, 16)
                sp.dma_start(dn_own[0:REST, bass.ds(n, 1), FULL, :].rearrange("p e d -> p (e d)"),
                             src[FULL * P:F, :]).then_inc(done, 16)

            def four(n):
                for u in range(4):
                    if not (isinstance(n, int) and 4 * n + u + 5 >= NT):
                        load_x(n * 4 + (u + 5), (u + 1) % 4)
                    if u % 2 == 0 and not known(n, 1):
                        store_x1(n * 4 + (u - 4), u // 2)
                    if u == 1:
                        load_gu(n + 1)
                    if u == 2:
                        load_dn(n + 1)

            load_x(0, 0)
            sp.dma_start(bias[:, 0:D], b_base.rearrange("(a o) -> a o", a=1).broadcast_to([P, D])).then_inc(s_cx, 16)
            for h in range(2):
                sp.dma_start(w_tok[h * SEQ:(h + 1) * SEQ, :, :],
                             cond.rearrange("(a t h) e -> h a t e", a=1, h=2)[h].broadcast_to([SEQ, NT, E])
                             ).then_inc(s_cx, 16)
            load_x(1, 1)
            load_x(2, 2)
            load_gu(0)
            load_x(3, 3)
            load_dn(0)
            load_x(4, 0)
            four(0)
            four(1)
            with sp.Fori(2, NT // 4 - 2) as n:
                four(n)
            four(NT // 4 - 2)
            sp.wait_ge(s_x1st[0], 16)
            for t in range(2):
                load_rows(fp, t, t, 0)
            four(NT // 4 - 1)

            def load_res(t, par, done):
                sp.dma_start(res[par][:], x_rows[bass.ds(t * P, P), :]).then_inc(done[par], 16)

            def store_base(t, par):
                sp.wait_ge(fp["y"], t + 1)
                sp.dma_start(base_dram[bass.ds(t * P, P), :], y_sb[par][:]).then_inc(s_bout[par], 16)

            store_x1(NT - 4, 0)
            store_x1(NT - 2, 1)
            load_gu(NE - 1)
            load_dn(NE - 1)
            for p in range(2):
                sp.wait_ge(s_x1st[p], 16 * (NT // 4))
            for t in range(2):
                load_res(t, t, s_bres)

            def step_p(t, par):
                load_rows(fp, t, par, 0)
                store_base(t - 2, par)
                load_res(t, par, s_bres)
            turns(sp, 2, NPRE, step_p)
            store_base(NPRE - 2, NPRE % 2)
            store_base(NPRE - 1, (NPRE - 1) % 2)

            def store_y(i, par):
                sp.wait_ge(fe["y"], i + 1)
                sp.dma_start(y_dram[bass.ds(i * P, P), :], y_sb[par][:]).then_inc(s_yst[par], 16)
            turns(sp, 0, NBLK - 2, store_y)

            def store_out(u, par, ready):
                sp.wait_ge(*ready)
                sp.dma_start(out_rows[bass.ds((u + NPRE) * P, P), :], y_sb[par][:]).then_inc(s_out[par], 16)

            def store_early(q, par):
                sp.wait_ge(s_emix, q * 2 + 2)
                sp.dma_start(out_rows[bass.ds(q * P, P), :], e_res[par][:]).then_inc(s_eout[par], 16)

            def load_base(q, par):
                if not known(q, 2):
                    sp.wait_ge(s_eout[par], half_of(q, par) * 16)
                sp.dma_start(e_res[par][:], base_dram[bass.ds(q * P, P), :]).then_inc(s_eres[par], 16)

            sp.wait_ge(fe["rt"], NBLK)
            load_rows(fs, NPRE, 0, NPRE)
            load_rows(fs, NPRE + 1, 1, NPRE)
            store_y(NBLK - 2, NBLK % 2)
            store_y(NBLK - 1, 1 - NBLK % 2)
            for t in range(NPRE, NPRE + 2):
                load_res(t, t % 2, s_res)
            for i in range(2):
                sp.wait_ge(s_bout[i], 16 * (NPRE // 2))

            def step_s(m, par, q, last_q):
                load_rows(fs, m + (NPRE + 2), par, NPRE)
                sp.wait_ge(fs["y"], m + 1)
                load_res(m + (NPRE + 2), par, s_res)
                if not known(m, 1):
                    store_out(m - 1, 1 - par, (s_mix, m * 2))
                if last_q:
                    store_early(*last_q)
                if q:
                    load_base(*q)
            with_early(sp, step_s)
            n = NT - NPRE
            store_out(n - 3, (n - 3) % 2, (s_mix, 2 * n - 4))
            store_out(n - 2, n % 2, (s_mix, 2 * n - 2))
            store_out(n - 1, (n - 1) % 2, (fs["y"], n))
            for i in range(2):
                sp.wait_ge(s_out[i], 16 * (n // 2))
                sp.wait_ge(s_eout[i], 16 * (NPRE // 2))

        @block.gpsimd
        def _(pool):
            n_pool = [0]

            def link(ins):
                n_pool[0] += 1
                ins.then_inc(s_pool, 1)
                pool.wait_ge(s_pool, n_pool[0])

            def before_dma():
                pool.tensor_tensor(spare[0:1, 1:2], spare[0:1, 0:1], spare[0:1, 0:1], ALU.add)

            link(pool.memset(spare[:], 0.0))
            link(pool.memset(ident[:], 1.0))
            pool.affine_select(out=ident[:], in_=ident[:], compare_op=ALU.is_equal, fill=0.0, base=0,
                               pattern=[[-1, P]], channel_multiplier=1).then_inc(s_ident, 1)

            small = dict(allow_small_or_imprecise_dtypes=True)
            pool.memset(g[:, F:], 0.0).then_inc(s_gz, 1)
            pool.iota(down_e[:], pattern=[[-1, E]], base=E, channel_multiplier=0, **small)
            pool.iota(step128[:], pattern=[[P, NT]], base=0, channel_multiplier=0, **small)
            pool.iota(iota_row[:], pattern=[[1, P]], base=0, channel_multiplier=0, **small)
            pool.iota(iota_blk[:], pattern=[[1, NBLKP]], base=0, channel_multiplier=0, **small)
            pool.iota(tok_id[:], pattern=[[P, NT]], base=0, channel_multiplier=1, **small)
            pool.memset(ones[:], 1.0)
            link(pool.memset(tri[:], 1.0))
            link(pool.affine_select(out=tri[:], in_=tri[:], compare_op=ALU.is_gt, fill=0.0, base=0,
                                    pattern=[[1, P]], channel_multiplier=-1))
            link(pool.memset(upto[:], 1.0))
            link(pool.affine_select(out=upto[:], in_=upto[:], compare_op=ALU.is_ge, fill=0.0, base=0,
                                    pattern=[[1, E], [-1, E]], channel_multiplier=0))
            pool.memset(mark[:, 0:PAD, :], 0.0)
            pool.memset(mark[:, PAD + NT, :], 0.0).then_inc(s_const, 1)

            def low_parts(n):
                for part, (own_ap, hi, lo) in enumerate(weight_parts(n)):
                    pool.wait_ge(s_whi, n * 4 + part + 1)
                    pool.tensor_tensor(lo, own_ap, hi.bitcast(F32), ALU.subtract).then_inc(s_wlo, 1)

            for n in range(NS):
                low_parts(n)
            with pool.Fori(NS, NE - 1) as n:
                low_parts(n)

            for p in range(2):
                pool.wait_ge(s_x1st[p], 16 * (NT // 4))
            pool.wait_ge(s_lg, NT)
            for buf in upto_tile:
                link(pool.memset(buf[:, 0:PAD, :], 0.0))
            pool.wait_ge(s_mark, 1)
            src, d, step = mark, 1, 0
            while d < NT:
                dst = upto_tile[step % 2]
                link(pool.tensor_tensor(dst[:, PAD:PAD + NT, :], src[:, PAD:PAD + NT, :],
                                        src[:, PAD - d:PAD + NT - d, :], ALU.add))
                src, d, step = dst, 2 * d, step + 1
            assert d == 2 * PAD and src is upto_tile[(step - 1) % 2]
            pool.tensor_copy(spare[0:1, 3:4], spare[0:1, 0:1]).then_inc(s_sums, 1)
            low_parts(NE - 1)

            pool.wait_ge(s_routed, 1)
            pool.wait_ge(fp["rt"], NPRE)

            def gather(i, par):
                if not known(i, 2):
                    pool.wait_ge(fe["rt"], i - 1)
                pool.tensor_copy(idx[par][:], perm_i[:, bass.ds(i, 1)]).then_inc(s_idx, 1)
                pool.wait_ge(s_idx, i + 1)
                before_dma()
                pool.indirect_dma_start(rows[par][:], None, x1_dram,
                                        bass.IndirectOffsetOnAxis(ap=idx[par][:, 0:1], axis=0)
                                        ).then_inc(fe["row"][par], 16)
            gather(0, 0)
            gather(1, 1)
            turns(pool, 2, NBLK, gather)

            pool.wait_ge(s_yst[0], 16 * ((NBLK + 1) // 2))
            pool.wait_ge(s_yst[1], 16 * (NBLK // 2))

            def gather_y(t, count, to, to_idx, counted, landed):
                for c in range(TOPK):
                    pool.tensor_copy(to_idx[c][:], slot_i[:, c, bass.ds(t, 1)]).then_inc(counted, 1)
                    pool.wait_ge(counted, count + (c + 1))
                    before_dma()
                    pool.indirect_dma_start(to[c][:], None, y_dram,
                                            bass.IndirectOffsetOnAxis(ap=to_idx[c][:, 0:1], axis=0)
                                            ).then_inc(landed, 16)

            def gather_late(t, par):
                if not known(t, NPRE + 2):
                    pool.wait_ge(s_mix, (t - (NPRE + 1)) * 2)
                gather_y(t, (t - NPRE) * 2, [pick[c][par] for c in range(TOPK)],
                         [pidx[c][par] for c in range(TOPK)], s_pidx, s_pick[par])

            def gather_early(q, par):
                if not known(q, 2):
                    pool.wait_ge(s_emix, q * 2 - 2)
                gather_y(q, q * 2, [pick[par] for pick in e_pick], [pi[par] for pi in e_pidx], s_epidx, s_epick[par])

            def step_y(m, par, q, _):
                if q:
                    gather_early(*q)
                gather_late(m + (NPRE + 2), par)
            gather_late(NPRE, 0)
            gather_late(NPRE + 1, 1)
            with_early(pool, step_y)

        def pe_turn_g(pe, s, i):
            pe.wait_ge(s["g"], i + 1)
            for c in range(FC):
                mm = pe.transpose(TB[:, c * P:(c + 1) * P], g[:, c * P:(c + 1) * P], ident[:])
            mm.then_inc(s["gT"], 1)

        def pe_gate_up(pe, s, e, rows_ready):
            pe.wait_ge(s["rtl"], rows_ready)
            for b, c, name in ((GB, 0, "G"), (UB, F, "U")):
                for k in range(K):
                    wh = gu_h[:, bass.ds(e, 1), k, c:c + F].rearrange("p e f -> p (e f)")
                    wl = gu_l[:, bass.ds(e, 1), k, c:c + F].rearrange("p e f -> p (e f)")
                    mm = three_pass(pe, b[:, 0:F], rt_h[:, k * P:(k + 1) * P], rt_l[:, k * P:(k + 1) * P],
                                    wh, wl, k == 0, k == K - 1)
                mm.then_inc(s[name], 1)

        def pe_turn_rows(pe, s, i, par):
            pe.wait_ge(s["row"][par], half_of(i, par) * 16 + 16)
            for k in range(K):
                mm = pe.transpose(XB[:, k * P:(k + 1) * P], rows[par][:, k * P:(k + 1) * P], ident[:])
            mm.then_inc(s["rt"], 1)

        def pe_down(pe, s, i, e, start, stop):
            pe.wait_ge(s["gTl"], i + 1)
            for c in range(FC):
                n = P if c < FULL else REST
                wh = dn_h[0:n, bass.ds(e, 1), c, :].rearrange("p e d -> p (e d)")
                wl = dn_l[0:n, bass.ds(e, 1), c, :].rearrange("p e d -> p (e d)")
                mm = three_pass(pe, YB[:, 0:D], gt_h[0:n, c * P:(c + 1) * P], gt_l[0:n, c * P:(c + 1) * P],
                                wh, wl, start and c == 0, stop and c == FC - 1)
            mm.then_inc(s["D"], 1)

        def act_gt(sc, s, i):
            sc.wait_ge(s["gT"], i + 1)
            sc.copy(gt_h[:], TB[:, 0:FC * P]).then_inc(s["gTh"], 1)

        def act_silu(sc, s, i):
            sc.wait_ge(s["G"], i + 1)
            if not known(i, 1):
                sc.wait_ge(s["g"], i)
            sc.activation(act[:], GB[:, 0:F], ACT.Silu).then_inc(s["act"], 1)

        def act_rows(sc, s, i):
            sc.wait_ge(s["rt"], i + 1)
            sc.copy(rt_h[:], XB[:, 0:D]).then_inc(s["rth"], 1)

        def dve_gt(v, s, i):
            v.wait_ge(s["gTh"], i + 1)
            v.tensor_tensor(gt_l[:], TB[:, 0:FC * P], gt_h[:].bitcast(F32), ALU.subtract).then_inc(s["gTl"], 1)

        def dve_g(v, s, i):
            v.wait_ge(s["act"], i + 1)
            v.wait_ge(s["U"], i + 1)
            if not known(i, 1):
                v.wait_ge(s["gT"], i)
            v.tensor_tensor(g[:, 0:F], UB[:, 0:F], act[:], ALU.mult).then_inc(s["g"], 1)

        def dve_rows(v, s, i):
            v.wait_ge(s["rth"], i + 1)
            v.tensor_tensor(rt_l[:], XB[:, 0:D], rt_h[:].bitcast(F32), ALU.subtract).then_inc(s["rtl"], 1)

        def pe_shared(pe, s, u, par, last=False, early=None, late=None, before=None):
            if not known(u, 1):
                pe_turn_g(pe, s, u * 2 - 1)
            elif before:
                before[0]()
            pe_gate_up(pe, s, 0, u + 1)
            if not known(u, 1):
                pe_down(pe, s, u * 2 - 1, 1, False, True)
            elif before:
                before[1]()
            if early:
                early()
            pe_turn_g(pe, s, u * 2)
            pe_gate_up(pe, s, 1, u + 1)
            if not last:
                pe_turn_rows(pe, s, u + 1, 1 - par)
            if late:
                late()
            if not known(u, 1):
                pe.wait_ge(s["y"], u)
            pe_down(pe, s, u * 2, 0, True, False)

        def pe_shared_end(pe, s, n):
            pe_turn_g(pe, s, 2 * n - 1)
            pe_down(pe, s, 2 * n - 1, 1, False, True)

        def act_shared(sc, s, u, last=False, mid=None, end=None, before=None):
            if not known(u, 1):
                act_gt(sc, s, u * 2 - 1)
            elif before:
                before[0]()
            act_silu(sc, s, u * 2)
            if before:
                before[1]()
            if mid:
                mid()
            act_gt(sc, s, u * 2)
            act_silu(sc, s, u * 2 + 1)
            if not last:
                act_rows(sc, s, u + 1)
            if end:
                end()

        @block.tensor
        def _(pe):
            pe.wait_ge(s_ident, 1)
            pe.wait_ge(s_cw, 16 * 3)
            for k in range(K):
                mm = pe.transpose(bank[3][:, k * E:(k + 1) * E], g_raw[:, k * P:(k + 1) * P], ident[0:E, 0:E])
            mm.then_inc(s_cwt, 1)
            for k in range(K):
                for o in range(K):
                    pe.transpose(bank[k][:, o * P:(o + 1) * P], base_raw[:, o, k * P:(k + 1) * P], ident[:])
                pe.transpose(bank[k][:, DX:DX + ER], a_raw[:, k * P:(k + 1) * P], ident[:])
            pe.wait_ge(s_cb, 16 * 4)
            for k in range(K):
                pe.transpose(bank[2][:, k * P:(k + 1) * P], b_raw[:, k, :], ident[:])
            pe.wait_ge(s_gate, 1)
            for k in range(K):
                for o in range(K):
                    pe.matmul(bank[k][:, D:DX], base_raw[:, o, k * P:(k + 1) * P], gate_t[:, o, :],
                              start=(o == 0), stop=(o == K - 1))
            for o in range(K):
                pe.matmul(bank[2][:, D:DX], b_raw[:, o, :], gate_t[:, o, :], start=(o == 0), stop=(o == K - 1))
            for o in range(K):
                mm = pe.matmul(bank[4][:, 0:E], b_col[:, o:o + 1].broadcast_to([P, P]), gate_t[:, o, :],
                               start=(o == 0), stop=(o == K - 1))
            mm.then_inc(s_cwf, 1)

            def turn_x(i, par):
                pe.wait_ge(s_xin[par], quarter_of(i, par) * 16 + 16)
                for k in range(K):
                    mm = pe.transpose(TX[:, k * P:(k + 1) * P], xin[par][:, k * P:(k + 1) * P], ident[:])
                mm.then_inc(s_tx, 1)

            def main(i, par, k):
                if k == 0 and not known(i, 4):
                    pe.wait_ge(s_lg, i - 3)
                mm = three_pass(pe, MAIN[par][:, 0:DX + ER], xt_h[par % 2][:, k * P:(k + 1) * P],
                                xt_l[par % 2][:, k * P:(k + 1) * P], wa_h[:, k, :], wa_l[:, k, :],
                                k == 0, k == K - 1)
                if k == K - 1:
                    mm.then_inc(s_main, 1)

            def turn_hw(i):
                pe.wait_ge(s_hw, i + 1)
                pe.transpose(THW[:, 0:P], hw[:], ident[:]).then_inc(s_thw, 1)

            def lora_out(i, par):
                pe.wait_ge(s_hwl, i + 1)
                three_pass(pe, MAIN[par][:, 0:DX], hw_h[:], hw_l[:], b_h[:], b_l[:], False, True,
                           skip=True).then_inc(s_p, 1)

            def step(i, par):
                pe.wait_ge(s_txl, i + 1)
                if not (isinstance(i, int) and i + 1 >= NT):
                    turn_x(i + 1, (par + 1) % 4)
                main(i, par, 0)
                if not known(i, 2):
                    lora_out(i - 2, (par - 2) % 4)
                if not known(i, 1):
                    turn_hw(i - 1)
                main(i, par, 1)

            pe.wait_ge(s_cwl, 1)
            turn_x(0, 0)
            pe.wait_ge(s_cwh, K + 1)
            pe.wait_ge(s_cwl, K + 1)
            for i in range(4):
                step(i, i)
            turns(pe, 4, NT - 1, step, 4)
            step(NT - 1, (NT - 1) % 4)
            lora_out(NT - 2, (NT - 2) % 4)
            turn_hw(NT - 1)
            pe_turn_rows(pe, fp, 0, 0)
            lora_out(NT - 1, (NT - 1) % 4)

            def rank():
                pe.wait_ge(s_const, 1)
                pe.wait_ge(s_sums, 1)
                W = (NT + 1) * E
                sums = upto_tile[(NT.bit_length() - 2) % 2]
                pe.matmul(RANK_B[:, 0:W], tri[:], mark[:, PAD:, :].rearrange("p t e -> p (t e)"),
                          start=True, stop=False)
                pe.matmul(RANK_B[:, 0:W], ones[:], sums[:, PAD - 1:, :].rearrange("p t e -> p (t e)"),
                          start=False, stop=True).then_inc(s_rank, 1)

            def perm(t, buf):
                pe.wait_ge(s_hot, t + 1)
                for c in range(TOPK):
                    mm = pe.matmul(PERM_B[:, 0:NBLKP], row_hot[c][buf][:], blk_hot[c][buf][:],
                                   start=isinstance(t, int) and t == 0 and c == 0,
                                   stop=isinstance(t, int) and t == NT - 1 and c == TOPK - 1)
                mm.then_inc(s_perm, 1)

            def perm_a(u):
                perm((u - HOT0) * 4, 0)
                perm((u - HOT0) * 4 + 1, 1)

            def perm_b(u):
                perm((u - HOT0) * 4 + 2, 2)
                perm((u - HOT0) * 4 + 3, 3)

            pe.wait_ge(s_wlo, 4 * NS)
            pe.wait_ge(s_lg, NT - 2)
            pe.wait_ge(s_gz, 1)
            for u in range(HOT0):
                pe_shared(pe, fp, u, u % 2, early=rank if u == RANK_AT else None)
            pe_shared(pe, fp, HOT0, HOT0 % 2, late=lambda: perm_a(HOT0))
            turns(pe, HOT0 + 1, HOT1, lambda u, par: pe_shared(
                pe, fp, u, par, early=lambda: perm_b(u - 1), late=lambda: perm_a(u)))
            pe_shared(pe, fp, NPRE - 1, (NPRE - 1) % 2, last=True, early=lambda: perm_b(NPRE - 2))

            pe_turn_rows(pe, fe, 0, 0)
            pe.wait_ge(s_wlo, 4 * NE)
            pe.wait_ge(s_blk, 1)

            def experts_from(b):
                _, es = nc.values_load_multi_w_load_instructions(
                    blk_e[0:1, bass.ds(b, TURN + 1)], engines=[mybir.EngineType.PE], min_val=NS, max_val=NE - 1,
                    skip_runtime_bounds_check_because="VectorE clips them to E - 1 and adds NS", bass_reorder=False)
                return lambda n: es[n]

            def e_down(i, e):
                if known(i, 1):
                    pe.wait_ge(fp["y"], NPRE)
                else:
                    pe.wait_ge(fe["y"], i)
                pe_down(pe, fe, i, e, True, True)

            def e_step(i, e_prev, e, turn_next):
                pe_turn_g(pe, fe, i - 1)
                pe_gate_up(pe, fe, e, i + 1)
                turn_next()
                e_down(i - 1, e_prev)

            expert = experts_from(0)
            pe_turn_g(pe, fp, 2 * NPRE - 1)
            pe_gate_up(pe, fe, expert(0), 1)
            pe_turn_rows(pe, fe, 1, 1)
            pe_down(pe, fp, 2 * NPRE - 1, 1, False, True)
            e_step(1, expert(0), expert(1), lambda: pe_turn_rows(pe, fe, 2, 0))
            n_turns = (NBLK - 3) // TURN
            assert TURN % 2 == 0
            with pe.Fori(0, n_turns) as j:
                expert = experts_from(j * TURN + 1)
                for d in range(TURN):
                    e_step(j * TURN + (2 + d), expert(d), expert(d + 1),
                           lambda: pe_turn_rows(pe, fe, j * TURN + (3 + d), 1 - d % 2))
            first = NBLK - 1 - TURN
            assert first <= n_turns * TURN + 1
            expert = experts_from(first)
            for i in range(n_turns * TURN + 2, NBLK):
                e_step(i, expert(i - 1 - first), expert(i - first),
                       (lambda: pe_turn_rows(pe, fe, i + 1, (i + 1) % 2)) if i + 1 < NBLK else
                       (lambda: pe_turn_rows(pe, fs, 0, 0)))

            n = NT - NPRE
            pe_shared(pe, fs, 0, 0, before=(lambda: pe_turn_g(pe, fe, NBLK - 1), lambda: e_down(NBLK - 1, expert(NBLK - 1 - first))),
                      late=lambda: pe.wait_ge(fe["y"], NBLK))
            turns(pe, 1, n - 1, lambda u, par: pe_shared(pe, fs, u, par))
            pe_shared(pe, fs, n - 1, (n - 1) % 2, last=True)
            pe_shared_end(pe, fs, n)

        @block.scalar
        def _(sc):
            sc.wait_ge(s_ident, 1)
            sc.activation(spare[0:1, 2:3], ident[0:1, 0:1], ACT.Silu)
            sc.wait_ge(s_cwt, 1)
            sc.copy(gate_t[:].rearrange("p k e -> p (k e)"), bank[3][:, 0:K * E]).then_inc(s_gate, 1)
            sc.wait_ge(s_cwf, 1)
            for k in range(K):
                sc.copy(wa_h[:, k, :], bank[k][:, 0:DX + ER]).then_inc(s_cwh, 1)
            sc.copy(bias[:, D:DX], bank[4][:, 0:E])
            sc.copy(b_h[:], bank[2][:, 0:DX]).then_inc(s_cwh, 1)

            def a_x(i, par):
                sc.wait_ge(s_tx, i + 1)
                if not known(i, 2):
                    sc.wait_ge(s_main, i - 1)
                sc.copy(xt_h[par % 2][:], TX[:, 0:D]).then_inc(s_txh, 1)

            def a_hw(i):
                sc.wait_ge(s_thw, i + 1)
                sc.copy(hw_h[:], THW[:, 0:P]).then_inc(s_hwh, 1)

            def high_parts(n, u):
                if u in (0, K):
                    if known(n, NE) and n == NE - 1:
                        sc.wait_ge(s_raw_end[u // K], 32)
                    else:
                        sc.wait_ge(s_raw[u // K], n * 32 + 32)
                for p, (own_ap, hi, _) in enumerate(weight_parts(n)):
                    if p == u or (u == K and p > K):
                        sc.copy(hi, own_ap).then_inc(s_whi, 1)

            def step(i, par):
                if not (isinstance(i, int) and i + 1 >= NT):
                    a_x(i + 1, par + 1)
                if not known(i, 1):
                    a_hw(i - 1)
            a_x(0, 0)
            for n in range(NS):
                for u in range(4):
                    step(4 * n + u, u)
                    if u <= K:
                        high_parts(n, u)
            with sc.Fori(NS, NT // 4 - 1) as n:
                for u in range(4):
                    step(n * 4 + u, u)
                    if u <= K:
                        high_parts(n, u)
            n_proj = NT // 4
            for u in range(4):
                step(NT - 4 + u, u)
                if u <= K:
                    high_parts(n_proj - 1, u)
            a_hw(NT - 1)
            act_rows(sc, fp, 0)

            act_shared(sc, fp, 0)

            def router_exp():
                sc.wait_ge(s_exp_in, 1)
                sc.activation(prob[:], pos[:], ACT.Exp).then_inc(s_exp, 1)
            act_shared(sc, fp, 1, mid=router_exp)
            for n in range(n_proj, NE):
                def some_high(*units):
                    for u in units:
                        high_parts(n, u)
                act_shared(sc, fp, n - n_proj + 2, mid=lambda: some_high(0, 1), end=lambda: some_high(2))
            turns(sc, NE - n_proj + 2, NPRE - 1, lambda u, par: act_shared(sc, fp, u))
            act_shared(sc, fp, NPRE - 1, last=True)

            def e_y(i, par):
                sc.wait_ge(fe["D"], i + 1)
                if known(i, 2):
                    sc.wait_ge(s_bout[par], 16 * (NPRE // 2))
                else:
                    sc.wait_ge(s_yst[par], half_of(i, par) * 16)
                sc.copy(y_sb[par][:], YB[:, 0:D]).then_inc(fe["y"], 1)

            def e_step(i, par):
                act_gt(sc, fe, i - 1)
                act_silu(sc, fe, i)
                if isinstance(i, int) and i == NBLK - 1:
                    act_rows(sc, fs, 0)
                else:
                    act_rows(sc, fe, i + 1)
                e_y(i - 1, 1 - par)
            act_rows(sc, fe, 0)
            act_gt(sc, fp, 2 * NPRE - 1)
            act_silu(sc, fe, 0)
            act_rows(sc, fe, 1)
            for i in (1, 2):
                e_step(i, i % 2)
            turns(sc, 3, NBLK - 1, e_step)
            e_step(NBLK - 1, (NBLK - 1) % 2)

            n = NT - NPRE
            act_shared(sc, fs, 0, before=(lambda: act_gt(sc, fe, NBLK - 1),
                                          lambda: e_y(NBLK - 1, (NBLK - 1) % 2)))
            turns(sc, 1, n - 1, lambda u, par: act_shared(sc, fs, u))
            act_shared(sc, fs, n - 1, last=True)
            act_gt(sc, fs, 2 * n - 1)

        @block.vector
        def _(v):
            for k in range(K):
                v.wait_ge(s_cwh, k + 1)
                v.tensor_tensor(wa_l[:, k, :], bank[k][:, 0:DX + ER], wa_h[:, k, :].bitcast(F32),
                                ALU.subtract).then_inc(s_cwl, 1)
            v.wait_ge(s_cwh, K + 1)
            v.tensor_tensor(b_l[:], bank[2][:, 0:DX], b_h[:].bitcast(F32), ALU.subtract).then_inc(s_cwl, 1)

            def v_x(i, par):
                v.wait_ge(s_txh, i + 1)
                v.tensor_tensor(xt_l[par % 2][:], TX[:, 0:D], xt_h[par % 2][:].bitcast(F32),
                                ALU.subtract).then_inc(s_txl, 1)

            def v_hw(i, par):
                v.wait_ge(s_main, i + 1)
                w = w_tok[:, bass.ds(i, 1), :].rearrange("p t (e r) -> p (t e) r", r=1).broadcast_to([P, E, RANK])
                v.scalar_tensor_tensor(out=hw[:].rearrange("p (e r) -> p e r", e=E),
                                       in0=MAIN[par][:, DX:DX + ER].rearrange("p (e r) -> p e r", e=E),
                                       scalar=LORA_SCALING, in1=w, op0=ALU.mult, op1=ALU.mult).then_inc(s_hw, 1)

            def v_hwl(i):
                v.wait_ge(s_hwh, i + 1)
                v.tensor_tensor(hw_l[:], THW[:, 0:P], hw_h[:].bitcast(F32), ALU.subtract).then_inc(s_hwl, 1)

            def v_x1(i, par):
                v.wait_ge(s_p, i + 1)
                if not known(i, 4) and par % 2 == 0:
                    v.wait_ge(s_x1st[par // 2], quarter_of(i, par) * 16)
                v.tensor_tensor(x1[par // 2][:, par % 2, :], MAIN[par][:, 0:D], bias[:, 0:D], ALU.add).then_inc(s_x1, 1)
                v.tensor_tensor(logits[:, bass.ds(i, 1), :].rearrange("p t e -> p (t e)"), MAIN[par][:, D:DX],
                                bias[:, D:DX], ALU.add).then_inc(s_lg, 1)

            def step(i, par):
                if not (isinstance(i, int) and i + 1 >= NT):
                    v_x(i + 1, par + 1)
                if not known(i, 2):
                    v_x1(i - 2, (par - 2) % 4)
                if not known(i, 1):
                    v_hwl(i - 1)
                v_hw(i, par)
            v_x(0, 0)
            v.wait_ge(s_cx, 16 * 3)
            for i in range(4):
                step(i, i)
            turns(v, 4, NT - 1, step, 4)
            step(NT - 1, (NT - 1) % 4)
            v_x1(NT - 2, (NT - 2) % 4)
            v_hwl(NT - 1)
            dve_rows(v, fp, 0)
            v_x1(NT - 1, (NT - 1) % 4)

            count = [0]

            def link(ins, cost=2):
                count[0] += 1
                ins.then_inc(s_r, 1)
                v.wait_ge(s_r, count[0])
                return cost

            def small(ins):
                return link(ins, cost=1)

            def over_e(a):
                return a[:].rearrange("p (t o) -> p t o", o=1).broadcast_to([P, NT, E])

            def routing():
                v.wait_ge(s_const, 1)
                for p in range(2):
                    v.wait_ge(s_x1st[p], 16 * (NT // 4))
                v.wait_ge(s_lg, NT)
                yield link(v.tensor_reduce(red[:], logits[:], AX.X, ALU.max))
                v.tensor_tensor(pos[:], logits[:], over_e(red), ALU.subtract).then_inc(s_exp_in, 1)
                yield 2
                v.wait_ge(s_exp, 1)
                yield link(v.tensor_reduce(red[:], prob[:], AX.X, ALU.add))
                yield link(v.reciprocal(red[:], red[:]))
                yield link(v.tensor_tensor(prob[:], prob[:], over_e(red), ALU.mult))
                for c, p in enumerate((prob, prob2)):
                    yield link(v.tensor_reduce(top_v[c][:], p[:], AX.X, ALU.max))
                    yield link(v.tensor_tensor(tmp[:], p[:], over_e(top_v[c]), ALU.is_equal))
                    yield link(v.tensor_tensor(tmp[:], tmp[:], down_e[:].rearrange("p (o e) -> p o e", o=1)
                                               .broadcast_to([P, NT, E]), ALU.mult))
                    yield link(v.tensor_reduce(red[:], tmp[:], AX.X, ALU.max))
                    yield link(v.tensor_tensor(hot[c][:], tmp[:], over_e(red), ALU.is_equal))
                    if c == 0:
                        yield link(v.scalar_tensor_tensor(out=prob2[:].rearrange("p t e -> p (t e)"),
                                                          in0=hot[0][:].rearrange("p t e -> p (t e)"), scalar=-2.0,
                                                          in1=prob[:].rearrange("p t e -> p (t e)"),
                                                          op0=ALU.mult, op1=ALU.add))
                v.tensor_tensor(mark[:, PAD:PAD + NT, :], hot[0][:], hot[1][:], ALU.add).then_inc(s_mark, 1)
                yield 1
                yield small(v.tensor_tensor(red[:], top_v[0][:], top_v[1][:], ALU.add))
                yield small(v.tensor_scalar(red[:], red[:], 1e-20, None, ALU.add))
                yield link(v.reciprocal(red[:], red[:]))
                for c in range(TOPK):
                    yield small(v.tensor_tensor(top_w[c][:], top_v[c][:], red[:], ALU.mult))
                    yield small(v.tensor_scalar(top_w[c][:], top_w[c][:], ROUTED_SCALE, None, ALU.mult))
                v.wait_ge(s_rank, 1)
                yield small(v.tensor_copy(nb[:], RANK_B[:, NT * E:(NT + 1) * E]))
                over = tmp[:].rearrange("p t e -> p (t e)").rearrange("p (e t) -> p e t", e=E)
                yield link(v.tensor_tensor(over, nb[:].rearrange("p (e o) -> p e o", o=1).broadcast_to([P, E, NT]),
                                           step128[:].rearrange("p (o t) -> p o t", o=1).broadcast_to([P, E, NT]),
                                           ALU.is_gt))
                yield link(v.tensor_reduce(nb[:], over, AX.X, ALU.add))
                yield small(v.tensor_tensor(ee[:], upto[:],
                                            nb[:].rearrange("p (o e) -> p o e", o=1).broadcast_to([P, E, E]), ALU.mult))
                yield small(v.tensor_reduce(bend[:], ee[:], AX.X, ALU.add))
                yield small(v.tensor_tensor(bbase[:], bend[:], nb[:], ALU.subtract))
                yield small(v.tensor_scalar(bbase[:], bbase[:], float(P), None, ALU.mult))
                yield link(v.tensor_tensor(pos[:], RANK_B[:, 0:NT * E].rearrange("p (t e) -> p t e", e=E),
                                           bbase[:].rearrange("p (o e) -> p o e", o=1).broadcast_to([P, NT, E]),
                                           ALU.add))
                for c in range(TOPK):
                    yield link(v.tensor_tensor(prob[:], pos[:], hot[c][:], ALU.mult))
                    yield link(v.tensor_reduce(slot_f[:, c, :], prob[:], AX.X, ALU.add))
                yield small(v.tensor_copy(slot_i[:], slot_f[:]))
                yield small(v.tensor_scalar(part_i[:], slot_i[:], 7, None, ALU.logical_shift_right))
                yield small(v.tensor_copy(blk_of[:], part_i[:]))
                yield small(v.tensor_scalar(part_i[:], slot_i[:], P - 1, None, ALU.bitwise_and))
                yield small(v.tensor_copy(row_of[:], part_i[:]))

            def block_experts():
                yield link(v.tensor_tensor(blk_cmp[:],
                                           iota_blk[0:1, :].rearrange("p (b o) -> p b o", o=1)
                                           .broadcast_to([1, NBLKP, E]),
                                           bend[0:1, :].rearrange("p (o e) -> p o e", o=1).broadcast_to([1, NBLKP, E]),
                                           ALU.is_ge), 4)
                yield link(v.tensor_reduce(blk_ef[:], blk_cmp[:], AX.X, ALU.add), 4)
                yield small(v.tensor_scalar(blk_ef[:], blk_ef[:], float(E - 1), None, ALU.min))
                v.tensor_scalar(blk_e[:], blk_ef[:], float(NS), None, ALU.add).then_inc(s_blk, 1)
                yield 1

            def wait_x(u, par):
                v.wait_ge(s_bres[par], half_of(u, par) * 16 + 16)

            def some(todo, cost):
                while cost > 0:
                    cost -= next(todo, cost)

            def final(s, u, par, counted):
                v.wait_ge(s["D"], u * 2 + 2)
                if not known(u, 2):
                    v.wait_ge(counted[par], half_of(u, par) * 16)
                v.tensor_tensor(y_sb[par][:], YB[:, 0:D], res[par][:], ALU.add).then_inc(s["y"], 1)

            def shared(s, u, par, counted, last=False, mid=None, end=None, early=None, late=None):
                if not known(u, 1):
                    dve_gt(v, s, u * 2 - 1)
                if early:
                    early()
                dve_g(v, s, u * 2)
                if not known(u, 1):
                    final(s, u - 1, 1 - par, counted)
                if mid:
                    mid()
                dve_gt(v, s, u * 2)
                if late:
                    late()
                dve_g(v, s, u * 2 + 1)
                if not last:
                    dve_rows(v, s, u + 1)
                if end:
                    end()

            def base_tile(u, par, **other):
                if not known(u, 1):
                    wait_x(u - 1, 1 - par)
                shared(fp, u, par, s_bout, **other)

            def with_math(u, todo, costs, last=False):
                base_tile(u, u % 2, last=last, **{
                    place: (lambda cost=cost: some(todo, cost)) for place, cost in zip(("early", "mid", "late", "end"), costs)})

            def hot_pair(u, k):
                for q in range(2):
                    hots(v, (u - HOT0) * 4 + (2 * k + q), 2 * k + q)

            todo = routing()
            for u in range(HOT0):
                with_math(u, todo, MATH[u])
            some(todo, 1000)

            def hot_tile(u, par):
                base_tile(u, par, mid=lambda: hot_pair(u, 0), end=lambda: hot_pair(u, 1))
            hot_tile(HOT0, HOT0 % 2)
            turns(v, HOT0 + 1, HOT1, hot_tile)

            def list_out():
                v.wait_ge(s_perm, NT)
                v.tensor_copy(perm_i[:], PERM_B[:, 0:NBLKP]).then_inc(s_routed, 1)
            assert HOT1 == NPRE - 1
            todo = block_experts()

            base_tile(HOT1, HOT1 % 2, last=True, early=lambda: some(todo, 4), mid=lambda: (list_out(), some(todo, 4)),
                      late=lambda: some(todo, 1000))

            def e_step(i, par):
                dve_gt(v, fe, i - 1)
                dve_g(v, fe, i)
                if isinstance(i, int) and i == NBLK - 1:
                    dve_rows(v, fs, 0)
                else:
                    dve_rows(v, fe, i + 1)
            dve_rows(v, fe, 0)
            dve_gt(v, fp, 2 * NPRE - 1)
            dve_g(v, fe, 0)
            dve_rows(v, fe, 1)
            wait_x(NPRE - 1, (NPRE - 1) % 2)
            final(fp, NPRE - 1, (NPRE - 1) % 2, s_bout)
            e_step(1, 1)
            turns(v, 2, NBLK - 1, e_step)
            e_step(NBLK - 1, (NBLK - 1) % 2)
            dve_gt(v, fe, NBLK - 1)

            def add_picks(to, picks, t, counted, n):
                for c in range(TOPK):
                    v.scalar_tensor_tensor(out=to[:], in0=picks[c][:], scalar=top_w[c][:, bass.ds(t, 1)],
                                           in1=to[:], op0=ALU.mult, op1=ALU.add).then_inc(counted, 1)
                    if c == 0:
                        v.wait_ge(counted, n + 1)

            def mix(u, par, to):
                v.wait_ge(s_pick[par], half_of(u, par) * 32 + 32)
                add_picks(to, [pick[c][par] for c in range(TOPK)], u + NPRE, s_mix, u * 2)

            def mix_early(q, par):
                v.wait_ge(s_eres[par], half_of(q, par) * 16 + 16)
                v.wait_ge(s_epick[par], half_of(q, par) * 32 + 32)
                add_picks(e_res[par], [e_pick[c][par] for c in range(TOPK)], q, s_emix, q * 2)

            def out_tile(m, par, _, last_q):
                v.wait_ge(s_res[par], half_of(m, par) * 16 + 16)
                shared(fs, m + 1, 1 - par, s_out,
                       early=None if known(m, 1) else lambda: mix(m - 1, 1 - par, y_sb[1 - par]),
                       late=(lambda: mix_early(*last_q)) if last_q else None)
            shared(fs, 0, 0, s_out)
            v.wait_ge(s_yst[0], 16 * ((NBLK + 1) // 2))
            v.wait_ge(s_yst[1], 16 * (NBLK // 2))
            with_early(v, out_tile)
            n = NT - NPRE

            def end():
                v.wait_ge(fs["y"], n - 1)
                mix(n - 2, n % 2, y_sb[n % 2])
                v.wait_ge(s_res[(n - 1) % 2], (n - 1) // 2 * 16 + 16)
                mix(n - 1, (n - 1) % 2, res[(n - 1) % 2])
            v.wait_ge(s_res[n % 2], (n - 2) // 2 * 16 + 16)
            shared(fs, n - 1, (n - 1) % 2, s_out, last=True, end=end,
                   early=lambda: mix(n - 3, (n - 3) % 2, y_sb[(n - 3) % 2]))
            dve_gt(v, fs, 2 * n - 1)
            v.wait_ge(s_mix, 2 * n)
            final(fs, n - 1, (n - 1) % 2, s_out)


_INS = ['x', 'cond_8', 'L0_cond_W_base', 'L0_cond_b_base', 'L0_cond_As', 'L0_cond_Bs', 'L0_ffn_gate_w',
        'L0_ffn_w_gate', 'L0_ffn_w_up', 'L0_ffn_w_down', 'L0_ffn_sw_gate', 'L0_ffn_sw_up', 'L0_ffn_sw_down']


def kernel(**inputs):
    import numpy as _np
    import concourse.bacc as _bacc
    from concourse import mybir as _mybir
    from concourse.bass_utils import run_bass_kernel_spmd as _run

    nc = _bacc.Bacc("TRN2", target_bir_lowering=False, num_devices=1)
    arrays, args = {}, []
    for name in _INS:
        a = _np.ascontiguousarray(inputs[name])
        arrays[f"in_{name}_dram"] = a
        args.append(nc.dram_tensor(f"in_{name}_dram", a.shape, _mybir.dt.from_np(a.dtype), kind="ExternalInput").ap())
    args.append(nc.dram_tensor("out_0_dram", inputs['x'].shape, _mybir.dt.float32, kind="ExternalOutput").ap())
    adaln_moe(nc, *args)
    r = _run(nc, [arrays], core_ids=[0])
    return r.results[0]["out_0_dram"]
```
